# Optimizing a Trainium2 kernel written in Bass

```python
import numpy as np
import jax
import jax.numpy as jnp

def _softmax(x, axis=-1):
    return jax.nn.softmax(x, axis=axis)

def _gelu(x):
    return jax.nn.gelu(x, approximate=True)

def _silu(x):
    return jax.nn.silu(x)

def _sigmoid(x):
    return jax.nn.sigmoid(x)

def _layernorm(x, axis=-1, eps=1e-05):
    m = jnp.mean(x, axis=axis, keepdims=True)
    v = jnp.var(x, axis=axis, keepdims=True)
    return (x - m) / jnp.sqrt(v + eps)

def _scatter_add(tgt, idx, src, axis=0):
    return tgt.at[idx].add(src)

def _segment_sum(src, seg, n):
    return jax.ops.segment_sum(src, seg, n)
kernel_name = 'mk_flamingo_gated_d2_seqx_r4_ad4a48'

def setup_inputs(seed: int=0):
    np.random.seed(seed)
    _w = jnp.asarray

    def _rec_inputs():
        import jax
        import jax.numpy as jnp
        _rk = jax.random.key(seed)
        x = 7.22e-05 + 1 * jax.random.normal(jax.random.fold_in(_rk, 1), (8, 512, 256), jnp.float32)
        _lenS = 512 - jax.random.randint(jax.random.fold_in(_rk, 7), (8,), 0, max(1, 512 // 4) + 1, jnp.int32)
        _lenS2 = 512 - jax.random.randint(jax.random.fold_in(_rk, 8), (8,), 0, max(1, 512 // 4) + 1, jnp.int32)
        _ctx_1024P = jax.random.normal(jax.random.fold_in(_rk, 11), (8, 16, 256), jnp.float32)
        _ctx_1024c = jax.random.dirichlet(jax.random.fold_in(_rk, 511), 0.3 * jnp.ones((16,), jnp.float32), (8, 512))
        _ctx_1024t = jnp.einsum('bsk,bkd->bsd', _ctx_1024c, _ctx_1024P)
        _ctx_1024t = _ctx_1024t * jax.lax.rsqrt(jnp.mean(jnp.square(_ctx_1024t)) + 1e-12) * 0.953939
        ctx_1024 = 4.13588e-05 + 0.999923 * (_ctx_1024t + 0.3 * jax.random.normal(jax.random.fold_in(_rk, 611), (8, 512, 256), jnp.float32))
        _validS = jnp.arange(512)[None, :] < _lenS[:, None]
        _validS2 = jnp.arange(512)[None, :] < _lenS2[:, None]
        _causal = jnp.tril(jnp.ones((512, 512), dtype=bool))
        mask_BxSxS2_bk1 = jnp.broadcast_to(_validS2[:, None, :], (8, 512, 512))
        _g = jax.random.normal(jax.random.fold_in(_rk, 9001), (2, 2), jnp.float32)
        _g = jnp.sign(_g) * jnp.maximum(jnp.abs(_g), 1.0) + (_g == 0) * 1.0
        g_xattn = _g[0]
        g_ffn = _g[1]
        return (x, ctx_1024, mask_BxSxS2_bk1, g_xattn, g_ffn)
    x, ctx_1024, mask_BxSxS2_bk1, g_xattn, g_ffn = _rec_inputs()

    def _L0_xattn_setup():
        import jax, jax.numpy as jnp
        import numpy as np
        BETA = 256
        NUM_HEADS = 16
        NORM = (BETA // NUM_HEADS) ** (-0.5)
        key = jax.random.key(seed)
        ks = jax.random.split(key, 6)
        B, N = (4, 512)
        D_in_q = D_in_k = D_in_v = 256
        D_out_k = D_out_v = 256
        q = jax.random.normal(ks[0], (B, N, D_in_q), dtype=jnp.float32)
        k = jax.random.normal(ks[1], (B, N, D_in_k), dtype=jnp.float32)
        v = jax.random.normal(ks[2], (B, N, D_in_v), dtype=jnp.float32)
        Wq = jax.random.normal(ks[3], (D_out_k, D_in_q), dtype=jnp.float32) * D_in_q ** (-0.5)
        Wk = jax.random.normal(ks[4], (D_out_k, D_in_k), dtype=jnp.float32) * D_in_k ** (-0.5)
        Wv = jax.random.normal(ks[5], (D_out_v, D_in_v), dtype=jnp.float32) * D_in_v ** (-0.5)
        return {'q': q, 'k': k, 'v': v, 'Wq': Wq, 'Wk': Wk, 'Wv': Wv}
    _L0_xattn_all = _L0_xattn_setup()
    _L0_xattn_in = {k: v for k, v in _L0_xattn_all.items() if k in ('Wq', 'Wk', 'Wv')}
    del _L0_xattn_all

    def _L0_ffn_setup():
        import jax, jax.numpy as jnp
        import numpy as np
        HIDDEN = 256
        NUM_EXPERTS = 16
        TOP_K = 6
        EPS = 1e-10
        key = jax.random.key(seed)
        k1, k2, k3, k4 = jax.random.split(key, 4)
        tokens = jax.random.normal(k1, (4, 512, HIDDEN), dtype=jnp.float32)
        bound = 1.0 / np.sqrt(HIDDEN)
        router_w = jax.random.uniform(k2, (NUM_EXPERTS, HIDDEN), jnp.float32, -bound, bound)
        router_b = jax.random.uniform(k3, (NUM_EXPERTS,), jnp.float32, -bound, bound)
        expert_w = jax.random.normal(k4, (NUM_EXPERTS, HIDDEN, HIDDEN), dtype=jnp.float32) / np.sqrt(HIDDEN)
        return {'tokens': tokens, 'router_w': router_w, 'router_b': router_b, 'expert_w': expert_w}
    _L0_ffn_all = _L0_ffn_setup()
    _L0_ffn_in = {k: v for k, v in _L0_ffn_all.items() if k in ('router_w', 'router_b', 'expert_w')}
    del _L0_ffn_all

    def _L1_xattn_setup():
        import jax, jax.numpy as jnp
        import numpy as np
        N, K, DIM_IN, DIM_Q, DIM_V = (4, 512, 256, 256, 256)
        key = jax.random.key(seed)
        ks = jax.random.split(key, 9)
        c_qk = np.sqrt(6.0 / (DIM_IN + DIM_Q))
        c_v = np.sqrt(6.0 / (DIM_IN + DIM_V))
        inp = {'query': jax.random.normal(ks[0], (N, K, DIM_IN), jnp.float32), 'key': jax.random.normal(ks[1], (N, K, DIM_IN), jnp.float32), 'value': jax.random.normal(ks[2], (N, K, DIM_IN), jnp.float32), 'mask': jnp.broadcast_to(jnp.triu(jnp.ones((K, K), bool), k=1), (N, K, K)), 'q_w': jax.random.uniform(ks[3], (DIM_Q, DIM_IN), jnp.float32, -c_qk, c_qk), 'q_b': jax.random.normal(ks[4], (DIM_Q,), jnp.float32) * 0.01, 'k_w': jax.random.uniform(ks[5], (DIM_Q, DIM_IN), jnp.float32, -c_qk, c_qk), 'k_b': jax.random.normal(ks[6], (DIM_Q,), jnp.float32) * 0.01, 'v_w': jax.random.uniform(ks[7], (DIM_V, DIM_IN), jnp.float32, -c_v, c_v), 'v_b': jax.random.normal(ks[8], (DIM_V,), jnp.float32) * 0.01}
        return inp
    _L1_xattn_all = _L1_xattn_setup()
    _L1_xattn_in = {k: v for k, v in _L1_xattn_all.items() if k in ('q_w', 'q_b', 'k_w', 'k_b', 'v_w', 'v_b')}
    del _L1_xattn_all

    def _L1_ffn_setup():
        import jax, jax.numpy as jnp
        import numpy as np
        NUM_HEADS = 16
        TOP_K = 2
        ROPE_BASE = 10000.0
        LN_EPS = 1e-05

        def _rope_sin_cos(S, D, dtype):
            inv_freq = 1.0 / ROPE_BASE ** (jnp.arange(0, D, 2, dtype=jnp.float32) / D)
            freqs = jnp.arange(S, dtype=jnp.float32)[:, None] * inv_freq[None, :]
            sin = jnp.sin(freqs).astype(dtype)[None, :, None, :]
            cos = jnp.cos(freqs).astype(dtype)[None, :, None, :]
            return (sin, cos)

        def _apply_rope(x, sin, cos):
            x1, x2 = (x[..., 0::2], x[..., 1::2])
            r1 = x1 * cos - x2 * sin
            r2 = x1 * sin + x2 * cos
            return jnp.stack([r1, r2], axis=-1).reshape(x.shape)

        def _layer_norm(x, w, b):
            mu = jnp.mean(x, axis=-1, keepdims=True)
            var = jnp.mean(jnp.square(x - mu), axis=-1, keepdims=True)
            return (x - mu) * jax.lax.rsqrt(var + LN_EPS) * w + b
        key = jax.random.key(seed)
        ks = jax.random.split(key, 8)
        B, S, E, NE = (2, 512, 256, 8)
        s = 0.02
        return {'x': jax.random.normal(ks[0], (B, S, E), dtype=jnp.float32), 'in_proj_w': jax.random.normal(ks[1], (3 * E, E), dtype=jnp.float32) * s, 'in_proj_b': jnp.zeros((3 * E,), dtype=jnp.float32), 'out_proj_w': jax.random.normal(ks[2], (E, E), dtype=jnp.float32) * s, 'out_proj_b': jnp.zeros((E,), dtype=jnp.float32), 'gate_w': jax.random.normal(ks[3], (NE, E), dtype=jnp.float32) * s, 'gate_b': jnp.zeros((NE,), dtype=jnp.float32), 'expert_w': jax.random.normal(ks[4], (NE, E, E), dtype=jnp.float32) * s, 'expert_b': jnp.zeros((NE, E), dtype=jnp.float32), 'ln1_w': jnp.ones((E,), dtype=jnp.float32), 'ln1_b': jnp.zeros((E,), dtype=jnp.float32), 'ln2_w': jnp.ones((E,), dtype=jnp.float32), 'ln2_b': jnp.zeros((E,), dtype=jnp.float32)}
    _L1_ffn_all = _L1_ffn_setup()
    _L1_ffn_in = {k: v for k, v in _L1_ffn_all.items() if k in ('in_proj_w', 'in_proj_b', 'out_proj_w', 'out_proj_b', 'gate_w', 'gate_b', 'expert_w', 'expert_b', 'ln1_w', 'ln1_b', 'ln2_w', 'ln2_b')}
    del _L1_ffn_all
    return {'x': x, 'ctx_1024': ctx_1024, 'mask_BxSxS2_bk1': mask_BxSxS2_bk1, 'g_xattn': g_xattn, 'g_ffn': g_ffn, 'L0_xattn_Wq': _L0_xattn_in['Wq'], 'L0_xattn_Wk': _L0_xattn_in['Wk'], 'L0_xattn_Wv': _L0_xattn_in['Wv'], 'L0_ffn_router_w': _L0_ffn_in['router_w'], 'L0_ffn_router_b': _L0_ffn_in['router_b'], 'L0_ffn_expert_w': _L0_ffn_in['expert_w'], 'L1_xattn_q_w': _L1_xattn_in['q_w'], 'L1_xattn_q_b': _L1_xattn_in['q_b'], 'L1_xattn_k_w': _L1_xattn_in['k_w'], 'L1_xattn_k_b': _L1_xattn_in['k_b'], 'L1_xattn_v_w': _L1_xattn_in['v_w'], 'L1_xattn_v_b': _L1_xattn_in['v_b'], 'L1_ffn_in_proj_w': _L1_ffn_in['in_proj_w'], 'L1_ffn_in_proj_b': _L1_ffn_in['in_proj_b'], 'L1_ffn_out_proj_w': _L1_ffn_in['out_proj_w'], 'L1_ffn_out_proj_b': _L1_ffn_in['out_proj_b'], 'L1_ffn_gate_w': _L1_ffn_in['gate_w'], 'L1_ffn_gate_b': _L1_ffn_in['gate_b'], 'L1_ffn_expert_w': _L1_ffn_in['expert_w'], 'L1_ffn_expert_b': _L1_ffn_in['expert_b'], 'L1_ffn_ln1_w': _L1_ffn_in['ln1_w'], 'L1_ffn_ln1_b': _L1_ffn_in['ln1_b'], 'L1_ffn_ln2_w': _L1_ffn_in['ln2_w'], 'L1_ffn_ln2_b': _L1_ffn_in['ln2_b']}

def reference(x, ctx_1024, mask_BxSxS2_bk1, g_xattn, g_ffn, L0_xattn_Wq, L0_xattn_Wk, L0_xattn_Wv, L0_ffn_router_w, L0_ffn_router_b, L0_ffn_expert_w, L1_xattn_q_w, L1_xattn_q_b, L1_xattn_k_w, L1_xattn_k_b, L1_xattn_v_w, L1_xattn_v_b, L1_ffn_in_proj_w, L1_ffn_in_proj_b, L1_ffn_out_proj_w, L1_ffn_out_proj_b, L1_ffn_gate_w, L1_ffn_gate_b, L1_ffn_expert_w, L1_ffn_expert_b, L1_ffn_ln1_w, L1_ffn_ln1_b, L1_ffn_ln2_w, L1_ffn_ln2_b):
    import jax
    import jax.numpy as jnp

    def _L0_xattn_ref(q, k, v, Wq, Wk, Wv):
        import jax, jax.numpy as jnp
        import numpy as np
        BETA = 256
        NUM_HEADS = 16
        NORM = (BETA // NUM_HEADS) ** (-0.5)
        qp = jax.nn.relu(jnp.einsum('bnd,od->bno', q, Wq))
        kp = jax.nn.relu(jnp.einsum('bnd,od->bno', k, Wk))
        vp = jax.nn.relu(jnp.einsum('bnd,od->bno', v, Wv))
        B, N, D = qp.shape
        dh = D // NUM_HEADS
        qh = qp.reshape(B, N, NUM_HEADS, dh)
        kh = kp.reshape(B, N, NUM_HEADS, dh)
        vh = vp.reshape(B, N, NUM_HEADS, vp.shape[-1] // NUM_HEADS)
        E = NORM * jnp.einsum('bqhd,bkhd->bhqk', qh, kh)
        A = jax.nn.softmax(E, axis=-1)
        out = jnp.einsum('bhqk,bkhd->bqhd', A, vh)
        return out.reshape(B, N, -1)

    def _L0_ffn_ref(tokens, router_w, router_b, expert_w):
        import jax, jax.numpy as jnp
        import numpy as np
        HIDDEN = 256
        NUM_EXPERTS = 16
        TOP_K = 6
        EPS = 1e-10
        B, S, H = tokens.shape
        E = expert_w.shape[0]
        T = B * S
        logits = jnp.einsum('bsh,eh->bse', tokens, router_w) + router_b
        probs = jax.nn.softmax(logits, axis=-1)
        top_p, top_i = jax.lax.top_k(probs, TOP_K)
        top_p = top_p / (jnp.sum(top_p, axis=-1, keepdims=True) + EPS)
        x = tokens.reshape(T, H)
        flat_i = top_i.reshape(T, TOP_K)
        flat_p = top_p.reshape(T, TOP_K)
        gate = jnp.zeros((T, E), dtype=flat_p.dtype)
        gate = gate.at[jnp.arange(T)[:, None], flat_i].add(flat_p)
        acc = jnp.maximum(jnp.sum(gate, axis=-1), EPS)
        out = jnp.zeros_like(x)
        for e in range(E):
            out = out + x @ expert_w[e] * gate[:, e:e + 1]
        out = (out / acc[:, None]).reshape(B, S, H)
        out = out + EPS * jnp.sum(top_p, axis=-1, keepdims=True)
        return out

    def _L1_xattn_ref(query, key, value, mask, q_w, q_b, k_w, k_b, v_w, v_b):
        import jax, jax.numpy as jnp
        import numpy as np
        N, K, DIM_IN, DIM_Q, DIM_V = (4, 512, 256, 256, 256)
        q = jnp.einsum('nkm,qm->nkq', query, q_w) + q_b
        k = jnp.einsum('nkm,qm->nkq', key, k_w) + k_b
        v = jnp.einsum('nkm,vm->nkv', value, v_w) + v_b
        scores = jnp.einsum('nqd,nkd->nqk', q, k) / jnp.sqrt(jnp.float32(DIM_Q))
        scores = jnp.where(mask, jnp.float32(-1000000000.0), scores)
        weights = jax.nn.softmax(scores, axis=2)
        y = jnp.einsum('nqk,nkv->nqv', weights, v)
        return y

    def _L1_ffn_ref(x, in_proj_w, in_proj_b, out_proj_w, out_proj_b, gate_w, gate_b, expert_w, expert_b, ln1_w, ln1_b, ln2_w, ln2_b):
        import jax, jax.numpy as jnp
        import numpy as np
        NUM_HEADS = 16
        TOP_K = 2
        ROPE_BASE = 10000.0
        LN_EPS = 1e-05

        def _rope_sin_cos(S, D, dtype):
            inv_freq = 1.0 / ROPE_BASE ** (jnp.arange(0, D, 2, dtype=jnp.float32) / D)
            freqs = jnp.arange(S, dtype=jnp.float32)[:, None] * inv_freq[None, :]
            sin = jnp.sin(freqs).astype(dtype)[None, :, None, :]
            cos = jnp.cos(freqs).astype(dtype)[None, :, None, :]
            return (sin, cos)

        def _apply_rope(x, sin, cos):
            x1, x2 = (x[..., 0::2], x[..., 1::2])
            r1 = x1 * cos - x2 * sin
            r2 = x1 * sin + x2 * cos
            return jnp.stack([r1, r2], axis=-1).reshape(x.shape)

        def _layer_norm(x, w, b):
            mu = jnp.mean(x, axis=-1, keepdims=True)
            var = jnp.mean(jnp.square(x - mu), axis=-1, keepdims=True)
            return (x - mu) * jax.lax.rsqrt(var + LN_EPS) * w + b
        B, S, E = x.shape
        H = NUM_HEADS
        D = E // H
        xh = x.reshape(B, S, H, D)
        sin, cos = _rope_sin_cos(S, D, x.dtype)
        q_in = _apply_rope(xh, sin, cos).reshape(B, S, E)
        k_in = q_in
        v_in = x
        Wq, Wk, Wv = jnp.split(in_proj_w, 3, axis=0)
        bq, bk, bv = jnp.split(in_proj_b, 3, axis=0)
        q = (q_in @ Wq.T + bq).reshape(B, S, H, D)
        k = (k_in @ Wk.T + bk).reshape(B, S, H, D)
        v = (v_in @ Wv.T + bv).reshape(B, S, H, D)
        scale = 1.0 / jnp.sqrt(jnp.asarray(D, dtype=x.dtype))
        scores = jnp.einsum('bqhd,bkhd->bhqk', q, k) * scale
        causal = jnp.tril(jnp.ones((S, S), dtype=bool))
        scores = jnp.where(causal[None, None], scores, jnp.asarray(-jnp.inf, dtype=scores.dtype))
        attn = jax.nn.softmax(scores, axis=-1)
        ctx = jnp.einsum('bhqk,bkhd->bqhd', attn, v).reshape(B, S, E)
        attn_out = ctx @ out_proj_w.T + out_proj_b
        x1 = _layer_norm(x + attn_out, ln1_w, ln1_b)
        gates = jax.nn.softmax(x1 @ gate_w.T + gate_b, axis=-1)
        _, top_idx = jax.lax.top_k(gates, TOP_K)
        top_gates = jnp.take_along_axis(gates, top_idx, axis=-1)
        expert_outputs = jnp.einsum('bsd,efd->bsef', x1, expert_w) + expert_b[None, None]
        sel = jnp.take_along_axis(expert_outputs, top_idx[..., None], axis=2)
        moe_out = jnp.sum(sel * top_gates[..., None], axis=2)
        return _layer_norm(x1 + moe_out, ln2_w, ln2_b)
    x = x + jnp.tanh(g_xattn[0]) * _L0_xattn_ref(_layernorm(x, axis=-1), ctx_1024, ctx_1024, L0_xattn_Wq, L0_xattn_Wk, L0_xattn_Wv)
    x = x + jnp.tanh(g_ffn[0]) * _L0_ffn_ref(_layernorm(x, axis=-1), L0_ffn_router_w, L0_ffn_router_b, L0_ffn_expert_w)
    x = x + jnp.tanh(g_xattn[1]) * _L1_xattn_ref(_layernorm(x, axis=-1), ctx_1024, ctx_1024, mask_BxSxS2_bk1, L1_xattn_q_w, L1_xattn_q_b, L1_xattn_k_w, L1_xattn_k_b, L1_xattn_v_w, L1_xattn_v_b)
    x = x + jnp.tanh(g_ffn[1]) * _L1_ffn_ref(_layernorm(x, axis=-1), L1_ffn_in_proj_w, L1_ffn_in_proj_b, L1_ffn_out_proj_w, L1_ffn_out_proj_b, L1_ffn_gate_w, L1_ffn_gate_b, L1_ffn_expert_w, L1_ffn_expert_b, L1_ffn_ln1_w, L1_ffn_ln1_b, L1_ffn_ln2_w, L1_ffn_ln2_b)
    return x

_drawn_inputs = setup_inputs


def setup_inputs(seed=0):
    import zlib

    import numpy as np

    out = dict(_drawn_inputs(seed))
    spreads = {'g_ffn': (-1.0, 0.2),
     'L1_ffn_in_proj_b': (0.0, 0.1),
     'L1_ffn_out_proj_b': (0.0, 0.1),
     'L1_ffn_gate_b': (0.0, 0.1),
     'L1_ffn_expert_b': (0.0, 0.1),
     'L1_ffn_ln1_w': (1.0, 0.2),
     'L1_ffn_ln1_b': (0.0, 0.1),
     'L1_ffn_ln2_w': (1.0, 0.2),
     'L1_ffn_ln2_b': (0.0, 0.1)}
    factors = {'L1_xattn_q_b': 30.438, 'L1_xattn_k_b': 64.0, 'L1_xattn_v_b': 6.178}
    for name, (base, spread) in spreads.items():
        noise = np.random.default_rng([zlib.crc32(name.encode()), seed]).standard_normal(out[name].shape)
        drawn = base * np.exp(spread * noise) if base else spread * noise
        out[name] = jnp.asarray(drawn.astype(out[name].dtype))
    for name, factor in factors.items():
        out[name] = (out[name] * factor).astype(out[name].dtype)
    return out
```

```python
import concourse.bass as bass
from concourse import mybir
from concourse.alu_op_type import AluOpType as ALU
from contextlib import ExitStack

F32 = mybir.dt.float32
F32R = mybir.dt.float32r
BF16 = mybir.dt.bfloat16
U8 = mybir.dt.uint8
ACT = mybir.ActivationFunctionType
AX = mybir.AxisListType

P = 128
NB, S, D = 8, 512, 256
TB = S // P
NT = NB * TB
KC = D // P
LN_EPS = 1e-5
BIG = 3.0e38


class Tally:

    def __init__(self, eng, sem, base=0):
        self.eng, self.sem, self.base, self.n = eng, sem, base, 0

    def done(self, instruction):
        self.n += 1
        instruction.then_inc(self.sem, 1)

    def wait(self):
        self.eng.wait_ge(self.sem, self.base + self.n)


def settle(eng, passed):
    eng.sem_inc(passed, 1)


class Kit:

    def __init__(self, nc, prefix, stack):
        self.nc, self.prefix, self.stack, self.sems = nc, prefix, stack, []
        stack.callback(self.release)

    def release(self):
        self.nc.clear_and_free_semaphores(self.sems)
        self.nc.all_engine_barrier()

    def sb(self, name, shape, dtype=F32):
        return self.stack.enter_context(self.nc.sbuf_tensor(f"{self.prefix}_{name}", shape, dtype))

    def ps(self, name, shape, dtype=F32):
        return self.stack.enter_context(self.nc.psum_tensor(f"{self.prefix}_{name}", shape, dtype))

    def sem(self, name):
        self.sems.append(self.nc.alloc_semaphore(f"{self.prefix}_{name}"))
        return self.sems[-1]


def three_pass(pe, out, lhs, rhs, first=True, last=True):
    n = len(lhs)
    for c in range(n):
        (lh, ll), (rh, rl) = lhs[c], rhs[c]
        for i, (a, b) in enumerate(((lh, rh), (lh, rl), (ll, rh))):
            made = pe.matmul(out, a, b, start=first and c == 0 and i == 0,
                             stop=last and c == n - 1 and i == 2)
    return made


def mha_phase(nc, shared, prefix, ins, layer1):
    X, ident, tg = shared["X"], shared["ident"], shared["tg"]
    H, DH = 16, D // 16
    NG, HG = 4, 4
    NU = 8
    NS = HG * TB
    AUG = 96
    VW = DH + 1
    LASTB = NB - 1
    with ExitStack() as stack:
        k = Kit(nc, prefix, stack)
        names = ["q", "k", "v"] + (["o"] if layer1 else [])
        w_hi = {n: k.sb(f"w{n}_hi", [P, KC, D], F32R) for n in names}
        w_lo = {n: k.sb(f"w{n}_lo", [P, KC, D], F32R) for n in names}
        xn = k.sb("xn", [P, TB, D])
        x_hi, x_lo = k.sb("x_hi", [P, KC, S], F32R), k.sb("x_lo", [P, KC, S], F32R)
        c_hi, c_lo = k.sb("c_hi", [P, KC, S], F32R), k.sb("c_lo", [P, KC, S], F32R)
        part = {n: (k.sb(f"{n}_hi", [P, S], F32R), k.sb(f"{n}_lo", [P, S], F32R)) for n in "qk"}
        QS = k.sb("QS", [P, NG, HG, S], F32R)
        KS = k.sb("KS", [P, NG, HG, S], F32R)
        V = k.sb("V", [P, TB, H, VW])
        PT = k.sb("PT", [P, NU, 2 * S])
        w_raw = {n: PT[:, i, 0:KC * D].rearrange("p (c n) -> p c n", c=KC) for i, n in enumerate(names)}
        OT = k.sb("OT", [P, S])
        nm = [k.sb(f"nm{i}", [P, NS]) for i in range(2)]
        MT = k.sb("MT", [NS, 2, P], F32R)
        rec = k.sb("rec", [P, TB, HG])
        stats, mv = k.sb("stats", [P, TB, 6]), k.sb("mv", [P, TB, 2])
        ve, mhalf, rstd = k.sb("ve", [P, TB]), k.sb("mhalf", [P, TB]), k.sb("rstd", [P, TB])
        if layer1:
            rope = k.sb("rope", [P, TB, D])
            r1, r2, r3 = (k.sb(n, [P, TB, D // 2]) for n in ("r1", "r2", "r3"))
            cos, sin = k.sb("cos", [P, TB, D // 2]), k.sb("sin", [P, TB, D // 2])
            bias = {n: k.sb(f"b{n}", [P, KC]) for n in "qk"}
            bv, bo = k.sb("bv", [P, D]), k.sb("bo", [P, D])
            ln_w, ln_b = k.sb("ln_w", [P, D]), k.sb("ln_b", [P, D])
            O = k.sb("O", [P, TB, D])
            o_hi, o_lo = k.sb("o_hi", [P, KC, S], F32R), k.sb("o_lo", [P, KC, S], F32R)
            y = k.sb("y", [P, TB, D])
            ystats, ymv = k.sb("ystats", [P, TB, 6]), k.sb("ymv", [P, TB, 2])
            yve, yrstd = k.sb("yve", [P, TB]), k.sb("yrstd", [P, TB])
            identb, mask_q, mask_k = (k.sb(n, [P, P], BF16) for n in ("identb", "mask_q", "mask_k"))
        else:
            c_raw = k.sb("c_raw", [P, KC, S])
            o_tmp = k.sb("o_tmp", [P, TB, HG * DH])
        st = k.ps("st", [P, 2, 2 * S])
        s2 = k.ps("s2", [P, 2, S])
        av = k.ps("av", [P, S])
        misc = k.ps("misc", [P, S])
        scratch = {n: [nc.dram_tensor(f"{prefix}_scratch_{n}{h}", [H // 2, 2, DH, S], F32).ap() for h in range(2)] for n in "qk"}
        m_scratch = nc.dram_tensor(f"{prefix}_scratch_m", [2, NS, P], F32).ap()

        sem = k.sem
        passed, x_rest_in = sem("passed"), sem("x_rest_in")
        w_in = [sem(f"w{n}_in") for n in names]
        w_hi_done, w_split, small_in = sem("w_hi_done"), sem("w_split"), sem("small_in")
        zeroed, ones_set, consts = sem("zeroed"), sem("ones_set"), sem("consts")
        c_in, c_hi_done, c_split = sem("c_in"), sem("c_hi_done"), sem("c_split")
        stats_ready, rstd_ready, xn_ready = sem("stats_ready"), sem("rstd_ready"), sem("xn_ready")
        misc_ready, misc_read, hi_done = sem("misc_ready"), sem("misc_read"), sem("hi_done")
        half_out, stack_in = sem("half_out"), [sem(f"stack_in{g}") for g in range(NG)]
        s_ready, max_done = sem("s_ready"), sem("max_done")
        st_ready, exp_done = sem("st_ready"), sem("exp_done")
        m_out, aug_in = sem("m_out"), [sem(f"aug_in{i}") for i in range(2)]
        av_done, ot_copied, o_added = sem("av_done"), sem("ot_copied"), sem("o_added")
        chain, pchain, vchain, rchain, ychain = (sem(n) for n in ("chain", "pchain", "vchain", "rchain", "ychain"))
        roped, rope_chain, n_kept, bo_added = sem("roped"), sem("rope_chain"), sem("n_kept"), sem("bo_added")
        ystats_ready, yrstd_ready, y_normed, x1_done = sem("ystats_ready"), sem("yrstd_ready"), sem("y_normed"), sem("x1_done")

        def schedule(first, last):
            t = [(0, 0, "V0"), (0, 1, "V1")]
            if layer1:
                nxt = [(0, 6, "xT0"), (0, 7, "xT1"), (1, 0, "q0"), (1, 1, "k0"), (1, 4, "cT0"), (1, 5, "cT1"), (3, 0, "q1"), (3, 1, "k1")]
                prev = [(0, 4, "oT0"), (0, 5, "oT1"), (2, 4, "op0"), (2, 6, "op1")]
            else:
                nxt = [(0, 4, "xT0"), (0, 5, "xT1"), (1, 0, "q0"), (1, 1, "k0"), (3, 0, "q1"), (3, 1, "k1")]
                prev = []
            for g in range(NG):
                if not (last and g == NG - 1):
                    t.append((g, 2, f"m{g}"))
                if not (first and g == 0):
                    t.append((g, 3, f"OT{g}"))
            t += [] if last else nxt
            t += [] if first else prev
            return sorted(t, key=lambda x: x[:2])

        PRO = (["cT0", "cT1"] if layer1 else []) + ["xT0", "xT1", "q0", "k0", "q1", "k1", "m"]
        TAIL = ["OT"] + (["oT0", "oT1", "op0", "op1"] if layer1 else [])
        HI = ("cT0", "cT1", "xT0", "xT1", "q0", "k0", "q1", "k1", "oT0", "oT1")

        class Order:

            def __init__(self, b, first=False, last=False):
                self.tasks = [n for _, _, n in schedule(first, last)]
                self.at = {(g, u): n for g, u, n in schedule(first, last)}
                lens = [len(schedule(True, False)), len(schedule(False, False))]
                his = [sum(n in HI for _, _, n in schedule(f, False)) for f in (True, False)]
                pro_hi = sum(n in HI for n in PRO)
                if first:
                    self.base, self.hbase = len(PRO), pro_hi
                else:
                    self.base = lens[1] * b + (len(PRO) + lens[0] - lens[1])
                    self.hbase = his[1] * b + (pro_hi + his[0] - his[1])

            def no(self, name):
                return self.base + self.tasks.index(name) + 1

            def hi(self, name):
                return self.hbase + [n for n in self.tasks if n in HI].index(name) + 1

        class Listed(Order):

            def __init__(self, tasks, base, hbase):
                self.tasks, self.base, self.hbase = tasks, base, hbase

        PROLOGUE = Listed(PRO, 0, 0)
        lastO = Order(LASTB, last=True)
        EPILOGUE = Listed(TAIL, lastO.base + len(lastO.tasks), lastO.hbase + sum(n in HI for n in lastO.tasks))

        def batches(eng, body):
            body(0, Order(0, first=True), True, False)
            with eng.Fori(1, LASTB) as b:
                body(b, Order(b), False, False)
            body(LASTB, lastO, False, True)

        def span(kc):
            return P * kc if layer1 else 0

        def cols(kcp):
            n0 = S - span(2 * kcp)
            at1 = n0 if layer1 else S
            return [(2 * kcp, 0, n0), (2 * kcp + 1, at1, S - span(2 * kcp + 1))]

        def tiles(b):
            return X[:, bass.ds(TB * b, TB), :]

        block = stack.enter_context(nc.Block())

        @block.sync
        def _(sp):
            for i, n in enumerate(names):
                sp.dma_start(w_raw[n], ins["w" + n].rearrange("(c p) n -> p c n", p=P)).then_inc(w_in[i], 16)
                if i == 0:
                    if layer1:
                        for dst, src in ((cos[:], ins["cos"].rearrange("(t p) n -> p t n", p=P)), (sin[:], ins["sin"].rearrange("(t p) n -> p t n", p=P)),
                                         (bias["q"][:], ins["bq"]), (bias["k"][:], ins["bk"]),
                                         (bv[:], ins["bv"].partition_broadcast(P)), (bo[:], ins["bo"].partition_broadcast(P)),
                                         (ln_w[:], ins["ln_w"].partition_broadcast(P)), (ln_b[:], ins["ln_b"].partition_broadcast(P))):
                            sp.dma_start(dst, src).then_inc(small_in, 16)
                    else:
                        sp.dma_start(c_raw[:], ins["ctxT"][0].rearrange("(c p) t -> p c t", p=P)).then_inc(c_in, 16)

            def store_half(b, h, ready):
                sp.wait_ge(misc_read, ready)
                settle(sp, passed)
                for g in (2 * h, 2 * h + 1):
                    if not (isinstance(b, int) and b == 0):
                        sp.wait_ge(stack_in[g], 64 * b)
                for n in "qk":
                    for i in range(2):
                        sp.dma_start(scratch[n][h][:, i], part[n][i][:].bitcast(F32)).then_inc(half_out, 16)
                sp.wait_ge(half_out, 64 * (2 * b + h + 1))

            def load_group(b, g):
                if not (isinstance(b, int) and b == 0):
                    sp.wait_ge(st_ready, NU * (NG * (b - 1) + g + 1))
                j0 = HG * (g % 2)
                for ten, n, runs in ((QS, "q", ((0, 0, 2), (2, 0, 1))), (KS, "k", ((0, 0, 1), (1, 0, 2)))):
                    src = scratch[n][g // 2]
                    for row, first, count in runs:
                        sp.dma_start(ten[row * DH:(row + count) * DH, g, :, :].bitcast(F32),
                                     src[j0:j0 + HG, first:first + count].rearrange("j i d t -> (i d) j t")).then_inc(stack_in[g], 16)

            if not layer1:
                sp.dma_start(X[:, TB:, :], ins["x"][1:].rearrange("b (t p) n -> p (b t) n", p=P)).then_inc(x_rest_in, 16)
            sp.wait_ge(zeroed, 2)
            store_half(0, 0, PROLOGUE.no("k0"))
            load_group(0, 0)
            load_group(0, 1)
            store_half(0, 1, PROLOGUE.no("k1"))
            load_group(0, 2)

            def batch(b, order, first, last):
                load_group(b, 3)
                if last:
                    return
                if not layer1:
                    sp.wait_ge(c_split, b + 1)
                    settle(sp, passed)
                    sp.dma_start(c_raw[:], ins["ctxT"][bass.ds(b + 1, 1)].rearrange("o (c p) t -> p (o c) t", p=P)).then_inc(c_in, 16)
                store_half(b + 1, 0, order.no("k0"))
                load_group(b + 1, 0)
                load_group(b + 1, 1)
                store_half(b + 1, 1, order.no("k1"))
                load_group(b + 1, 2)
            batches(sp, batch)

        @block.tensor
        def _(pe):
            def pairs(hi, lo, cut):
                return [(hi[:, c, cut], lo[:, c, cut]) for c in range(KC)]

            def misc_free(order, name):
                n = order.no(name) - 1
                if not (isinstance(n, int) and n == 0):
                    pe.wait_ge(misc_read, n)

            def projection(n, h):
                hi, lo = (x_hi, x_lo) if n == "q" or layer1 else (c_hi, c_lo)
                return three_pass(pe, misc[:], pairs(w_hi[n], w_lo[n], slice(h * P, h * P + P)), pairs(hi, lo, slice(0, S)))

            def run(name, order, b):
                misc_free(order, name)
                kind, i = name[:-1], int(name[-1])
                if kind in ("xT", "cT"):
                    src = xn
                    if kind == "xT":
                        if layer1:
                            src = rope
                            pe.wait_ge(roped, 2 * (b + 2))
                        else:
                            pe.wait_ge(xn_ready, b + 2)
                    else:
                        pe.wait_ge(xn_ready, b + 2)
                    for t in range(TB):
                        made = pe.transpose(misc[:, t * P:(t + 1) * P], src[:, t, i * P:(i + 1) * P], ident[:])
                elif kind in ("q", "k"):
                    if kind == "k" and not layer1:
                        pe.wait_ge(c_split, b + 2)
                    made = projection(kind, i)
                elif kind == "V":
                    for j in range(2):
                        t = 2 * i + j
                        made = three_pass(pe, misc[:, j * D:(j + 1) * D], pairs(c_hi, c_lo, slice(t * P, (t + 1) * P)),
                                          pairs(w_hi["v"], w_lo["v"], slice(0, D)))
                elif kind == "oT":
                    for t in range(TB):
                        made = pe.transpose(misc[:, t * P:(t + 1) * P], O[:, t, i * P:(i + 1) * P], ident[:])
                elif kind == "op":
                    for j in range(2):
                        t = 2 * i + j
                        made = three_pass(pe, misc[:, j * D:(j + 1) * D], pairs(o_hi, o_lo, slice(t * P, (t + 1) * P)),
                                          pairs(w_hi["o"], w_lo["o"], slice(0, D)))
                made.then_inc(misc_ready, 1)

            def scores(G, slot, s):
                j, t = divmod(s, TB)
                n = P * (t + 1) if layer1 else S
                pe.wait_ge(max_done, NS * G + s + 1)
                made = pe.matmul(s2[:, s % 2, 0:n], QS[0:AUG, slot, j, t * P:(t + 1) * P], KS[0:AUG, slot, j, 0:n],
                                 start=True, stop=not layer1)
                if layer1:
                    made = pe.matmul(s2[:, s % 2, t * P:n], identb[:], mask_q[:], start=False, stop=True)
                made.then_inc(s_ready, 1)

            def scores_t(G, g, u):
                kcp, j = divmod(u, HG)
                pe.wait_ge(exp_done, NU * G + u + 1)
                for kc, at, n in cols(kcp):
                    made = pe.matmul(st[:, u % 2, at:at + n], KS[0:AUG + 2, g, j, kc * P:(kc + 1) * P], QS[0:AUG + 2, g, j, S - n:S],
                                     start=True, stop=not layer1)
                    if layer1:
                        made = pe.matmul(st[:, u % 2, at:at + P], identb[:], mask_k[:], start=False, stop=True)
                made.then_inc(st_ready, 1)

            def values(G, g, kcp, i):
                if i == 0:
                    pe.wait_ge(exp_done, NU * G + HG * (kcp + 1) + 2)
                kc, at, n = cols(kcp)[i]
                for j in range(HG):
                    made = pe.matmul(av[32 * j:32 * j + VW, S - n:S], V[:, kc, HG * g + j, :], PT[:, HG * kcp + j, at:at + n],
                                     start=kc == 0, stop=kc == TB - 1, skip_group_check=True)
                if i == 1:
                    made.then_inc(av_done, 1)

            def run_m(order, name, b, g):
                misc_free(order, name)
                pe.wait_ge(max_done, NS * (NG * b + g + 2) + 2)
                pe.transpose(misc[0:NS, 0:P], nm[(g + 1) % 2][:], ident[:]).then_inc(misc_ready, 1)

            def run_ot(order, name, b, g):
                misc_free(order, name)
                pe.wait_ge(ot_copied, NG * b + g)
                for t in range(TB):
                    made = pe.transpose(misc[:, t * P:(t + 1) * P], OT[:, t * P:(t + 1) * P], ident[:])
                made.then_inc(misc_ready, 1)

            pe.wait_ge(w_split, len(names))
            for name in PRO[:-1]:
                run(name, PROLOGUE, -1)
            pe.wait_ge(zeroed, 2)
            pe.wait_ge(consts, 1)
            for G in range(2):
                pe.wait_ge(stack_in[G], 64)
                for s in range(NS):
                    scores(G, G, s)
                if G == 0:
                    run_m(PROLOGUE, "m", 0, -1)

            def task(order, b, g, u):
                name = order.at.get((g, u))
                if name:
                    if name[0] == "m":
                        run_m(order, name, b, g)
                    elif name[:2] == "OT":
                        run_ot(order, name, b, g)
                    else:
                        run(name, order, b)

            def batch(b, order, first, last):
                for g in range(NG):
                    G = NG * b + g
                    ahead = not (last and g >= 2)
                    slot = (g + 2) % NG
                    pe.wait_ge(aug_in[g % 2], 16 * (2 * b + g // 2 + 1))
                    if g == 0 and first:
                        pe.wait_ge(ones_set, 1)
                    for u in range(NU):
                        scores_t(G, g, u)
                        if ahead:
                            if u == 0:
                                pe.wait_ge(stack_in[slot], 64 * (b + 1 + (g + 2) // NG))
                            scores(G + 2, slot, 2 * u)
                        if u == 5:
                            if not (first and g == 0):
                                pe.wait_ge(ot_copied, G)
                            if g == 0:
                                pe.wait_ge(misc_read, order.no("V1"))
                            values(G, g, 0, 0)
                        elif u == 1 and not (first and g == 0):
                            values(G - 1, (g - 1) % NG, 1, 0)
                        if ahead:
                            scores(G + 2, slot, 2 * u + 1)
                        if u == 5:
                            values(G, g, 0, 1)
                        elif u == 1 and not (first and g == 0):
                            values(G - 1, (g - 1) % NG, 1, 1)
                        task(order, b, g, u)

            batches(pe, batch)
            for i in range(2):
                values(NG * NB - 1, NG - 1, 1, i)
            for name in TAIL:
                if name == "OT":
                    run_ot(EPILOGUE, "OT", NB, 0)
                else:
                    run(name, EPILOGUE, LASTB)

        @block.vector
        def _(dve):
            LEN = shared["lens"].get(prefix, (0, 0))

            def norm_stats(b, link):
                for t in range(TB):
                    link.done(dve.bn_stats(stats[:, t, :], X[:, bass.ds(TB * b + t, 1), :].rearrange("p o n -> p (o n)")))
                link.wait()
                settle(dve, passed)
                for t in range(TB):
                    made = dve.bn_aggr(mv[:, t, :], stats[:, t, :])
                made.then_inc(stats_ready, 1)

            def norm_apply(b):
                dve.wait_ge(rstd_ready, b + 1)
                if layer1 and not (isinstance(b, int) and b == 0):
                    dve.wait_ge(n_kept, b)
                for t in range(TB):
                    made = dve.tensor_scalar(xn[:, t, :], X[:, bass.ds(TB * b + t, 1), :].rearrange("p o n -> p (o n)"),
                                             mv[:, t, 0:1], rstd[:, t:t + 1], ALU.subtract, ALU.mult)
                made.then_inc(xn_ready, 1)

            def pair_view(ten, odd):
                return ten[:].rearrange("p t (n two) -> p t n two", two=2)[:, :, :, odd]

            def rotate_second(b):
                dve.wait_ge(xn_ready, b + 1)
                dve.tensor_tensor(r2[:], pair_view(xn, 0), sin[:], ALU.mult).then_inc(rope_chain, 1)
                dve.tensor_tensor(y[:, :, 0:D // 2], pair_view(xn, 1), cos[:], ALU.mult).then_inc(rope_chain, 1)
                dve.wait_ge(rope_chain, 2 * (b + 1))
                dve.tensor_tensor(pair_view(rope, 1), r2[:], y[:, :, 0:D // 2], ALU.add).then_inc(roped, 1)

            def low_part(order, name, dst_hi, dst_lo, op=None, value=None):
                dve.wait_ge(hi_done, order.hi(name))
                if op is None:
                    made = dve.tensor_tensor(dst_lo, misc[:], dst_hi.bitcast(F32), ALU.subtract)
                else:
                    made = dve.scalar_tensor_tensor(dst_lo, misc[:], value, dst_hi.bitcast(F32), op, ALU.subtract)
                made.then_inc(misc_read, 1)

            def minus_max_parts(order, name, b, g, link):
                dve.wait_ge(misc_ready, order.no(name))
                if name != "m":
                    dve.wait_ge(m_out, 16 * (NG * b + g + 1))
                link.done(dve.tensor_copy(MT[:, 0, :], misc[0:NS, 0:P]))
                link.wait()
                dve.tensor_tensor(MT[:, 1, :], misc[0:NS, 0:P], MT[:, 0, :].bitcast(F32), ALU.subtract).then_inc(misc_read, 1)

            def outputs(order, name, G, go, link, single):
                dve.wait_ge(misc_ready, order.no(name))
                view = misc[:].rearrange("p (t j c) -> p t j c", t=TB, j=HG)
                link.done(dve.reciprocal(rec[:], view[:, :, :, DH]))
                link.wait()
                if layer1:
                    dst = O[:, :, HG * DH * go:HG * DH * (go + 1)]
                else:
                    link.done(dve.tensor_scalar(rec[:], rec[:], tg[:, 0:1], None, ALU.mult))
                    link.wait()
                    if not (isinstance(G, int) and G == 0):
                        dve.wait_ge(o_added, G)
                    dst = o_tmp[:]
                dve.tensor_tensor(dst.rearrange("p t (j c) -> p t j c", j=HG), view[:, :, :, 0:DH],
                                  rec[:].unsqueeze(3).to_broadcast([P, TB, HG, DH]), ALU.mult).then_inc(misc_read, 1)

            def take(name, order, b, link):
                kind, i = name[:-1], int(name[-1])
                if kind == "xT":
                    low_part(order, name, x_hi[:, i, :], x_lo[:, i, :])
                elif kind == "cT":
                    low_part(order, name, c_hi[:, i, :], c_lo[:, i, :])
                elif kind == "oT":
                    low_part(order, name, o_hi[:, i, :], o_lo[:, i, :])
                elif kind in ("q", "k"):
                    op, value = (ALU.add, bias[kind][:, i:i + 1]) if layer1 else (ALU.max, 0.0)
                    low_part(order, name, part[kind][0][:], part[kind][1][:], op, value)
                elif kind == "V":
                    dve.wait_ge(misc_ready, order.no(name))
                    dst = V[:, 2 * i:2 * i + 2, :, 0:DH]
                    src = misc[:].rearrange("p (t h c) -> p t h c", t=2, h=H)
                    if layer1:
                        made = dve.tensor_tensor(dst, src, bv[:].rearrange("p (h c) -> p h c", h=H).unsqueeze(1).to_broadcast([P, 2, H, DH]), ALU.add)
                    else:
                        made = dve.tensor_scalar(dst, src, 0.0, None, ALU.max)
                    made.then_inc(misc_read, 1)
                elif kind == "op":
                    dve.wait_ge(misc_ready, order.no(name))
                    if i == 0:
                        dve.wait_ge(x1_done, b)
                        dve.wait_ge(bo_added, b)
                    for j in range(2):
                        t = 2 * i + j
                        made = dve.tensor_tensor(y[:, t, :], misc[:, j * D:(j + 1) * D],
                                                 X[:, bass.ds(TB * (b - 1) + t, 1), :].rearrange("p o n -> p (o n)"), ALU.add)
                        made.then_inc(*((misc_read, 1) if j else (chain, 1)))
                    link.n += 1
                    link.wait()
                    dve.wait_ge(misc_read, order.no(name))
                    for j in range(2):
                        link.done(dve.bn_stats(ystats[:, 2 * i + j, :], y[:, 2 * i + j, :]))
                    link.wait()
                    settle(dve, passed)
                    for j in range(2):
                        made = dve.bn_aggr(ymv[:, 2 * i + j, :], ystats[:, 2 * i + j, :])
                    made.then_inc(ystats_ready, 1)

            def first_norm(b):
                dve.wait_ge(yrstd_ready, b)
                for t in range(TB):
                    made = dve.tensor_scalar(y[:, t, :], y[:, t, :], ymv[:, t, 0:1], yrstd[:, t:t + 1], ALU.subtract, ALU.mult)
                made.then_inc(y_normed, 1)

            def maxima(G, par, s):
                n = P * (s % TB + 1) if layer1 else S
                dve.wait_ge(s_ready, NS * G + s + 1)
                dve.tensor_reduce(nm[par][:, s:s + 1], s2[:, s % 2, 0:n], axis=AX.X, op=ALU.max, negate=True).then_inc(max_done, 1)

            def wait_half(b, h):
                if not (isinstance(b, int) and b == 0 and h == 0):
                    dve.wait_ge(half_out, 64 * (2 * b + h))

            link = Tally(dve, chain)
            dve.sem_inc(max_done, 2)
            if layer1:
                dve.sem_inc(x1_done, 1)
            norm_stats(0, link)
            for i, n in enumerate(names):
                dve.wait_ge(w_hi_done, i + 1)
                dve.tensor_tensor(w_lo[n][:], w_raw[n], w_hi[n][:].bitcast(F32), ALU.subtract).then_inc(w_split, 1)
            norm_apply(0)
            if layer1:
                dve.wait_ge(small_in, 128)
                rotate_second(0)
            link.done(dve.memset(V[:, :, :, DH:], 1.0))
            link.done(dve.memset(av[:], 0.0))
            for name in PRO[:-1]:
                if name[0] in "qk":
                    wait_half(0, int(name[1]))
                take(name, PROLOGUE, 0, link)
            for G in range(2):
                for s in range(NS):
                    maxima(G, G, s)
                if G == 0:
                    minus_max_parts(PROLOGUE, "m", 0, -1, link)
            starts = [link.n]

            def batch(b, order, first, last):
                if first:
                    base = starts[0]
                else:
                    base = starts[0] + LEN[0] + (b - 1) * LEN[1] if isinstance(b, int) else LEN[1] * b + (starts[0] + LEN[0] - LEN[1])
                link = Tally(dve, chain, base)
                for g in range(NG):
                    G = NG * b + g
                    for u in range(NU):
                        if not (last and g >= 2):
                            maxima(G + 2, g % 2, 2 * u)
                            maxima(G + 2, g % 2, 2 * u + 1)
                        name = order.at.get((g, u))
                        if name:
                            if name[0] == "m":
                                minus_max_parts(order, name, b, g, link)
                            elif name[:2] == "OT":
                                outputs(order, name, G - 1, (g - 1) % NG, link, first)
                            else:
                                if name[0] in "qk":
                                    wait_half(b + 1, int(name[1]))
                                if name == "V0" and not first:
                                    dve.wait_ge(av_done, 2 * G - 1)
                                if name == "V1" and not first:
                                    dve.wait_ge(av_done, 2 * G)
                                take(name, order, b, link)
                        if not last:
                            if g == 0 and u == 0:
                                if first and not layer1:
                                    dve.wait_ge(x_rest_in, 16)
                                norm_stats(b + 1, link)
                            if g == 0 and u == 3 - layer1:
                                norm_apply(b + 1)
                            if layer1 and g == 0 and u == 4:
                                if not first:
                                    dve.wait_ge(x1_done, b)
                                rotate_second(b + 1)
                        if layer1 and not first and g == 3 and u == 4:
                            first_norm(b)
                if first:
                    assert link.n == LEN[0], f"{prefix} first chain {link.n}"
                elif not last:
                    assert link.n == LEN[1], f"{prefix} chain {link.n}"
                starts.append(link)
            batches(dve, batch)
            link = starts[-1]
            outputs(EPILOGUE, "OT", NG * NB - 1, NG - 1, link, False)
            for name in TAIL[1:]:
                take(name, EPILOGUE, NB, link)
            if layer1:
                first_norm(NB)

        @block.scalar
        def _(act):
            act.sem_inc(exp_done, 2)
            for i, n in enumerate(names):
                act.wait_ge(w_in[i], 16)
                act.activation(w_hi[n][:], w_raw[n], ACT.Copy).then_inc(w_hi_done, 1)

            def context_high(b):
                act.wait_ge(c_in, 16 * (b + 1))
                act.activation(c_hi[:], c_raw[:], ACT.Copy).then_inc(c_hi_done, 1)

            def keep_n(b):
                act.wait_ge(xn_ready, b + 1)
                act.activation(tiles(b).rearrange("p t n -> p (t n)"), xn[:].rearrange("p t n -> p (t n)"), ACT.Copy).then_inc(n_kept, 1)

            def high_part(name, order, b):
                kind, i = name[:-1], int(name[-1])
                act.wait_ge(misc_ready, order.no(name))
                func, kw = ACT.Copy, {}
                if kind in ("q", "k"):
                    if not (isinstance(b, int) and b == 0 and i == 0):
                        act.wait_ge(half_out, 64 * (2 * b + i))
                    dst = part[kind][0][:]
                    func, kw = (ACT.Identity, dict(bias=bias[kind][:, i:i + 1])) if layer1 else (ACT.Relu, {})
                else:
                    dst = {"xT": x_hi, "cT": c_hi}[kind][:, i, :] if kind != "oT" else o_hi[:, i, :]
                act.activation(dst, misc[:], func, **kw).then_inc(hi_done, 1)

            def exponentials(G, u, first):
                kcp, j = divmod(u, HG)
                act.wait_ge(st_ready, NU * G + u + 1)
                if not first:
                    act.wait_ge(av_done, 2 * G - 1 + kcp)
                n = sum(c[2] for c in cols(kcp))
                act.activation(PT[:, u, 0:n], st[:, u % 2, 0:n], ACT.Exp, scale=DH ** -0.5).then_inc(exp_done, 1)

            if layer1:
                act.wait_ge(small_in, 128)
                keep_n(0)
            else:
                context_high(0)
            for name in PRO[:-1]:
                high_part(name, PROLOGUE, 0)

            def batch(b, order, first, last):
                for g in range(NG):
                    G = NG * b + g
                    for u in range(NU):
                        exponentials(G, u, first and g == 0)
                        name = order.at.get((g, u))
                        if name in HI:
                            high_part(name, order, b + 1)
                        if u == 2 and not (first and g == 0):
                            act.wait_ge(av_done, 2 * G)
                            if not (first and g == 1):
                                act.wait_ge(misc_ready, order.no(f"OT{g - 1}") if g else prev_ot(b))
                            act.activation(OT[:], av[:], ACT.Copy).then_inc(ot_copied, 1)
                        if not last and g == 0:
                            if not layer1 and u == 3:
                                act.wait_ge(misc_ready, order.no("V1"))
                                context_high(b + 1)
                            if layer1 and u == 3:
                                keep_n(b + 1)

            def prev_ot(b):
                if isinstance(b, int) and b == 0:
                    raise AssertionError
                first_len, mid = [n for _, _, n in schedule(True, False)], [n for _, _, n in schedule(False, False)]
                back_first, back_mid = len(first_len) - first_len.index("OT3"), len(mid) - mid.index("OT3")
                assert back_first == back_mid
                return Order(b).base - back_mid + 1
            batches(act, batch)
            act.wait_ge(av_done, 2 * NG * NB)
            act.wait_ge(misc_ready, lastO.no("OT3"))
            act.activation(OT[:], av[:], ACT.Copy).then_inc(ot_copied, 1)
            for name in TAIL:
                if name in HI:
                    high_part(name, EPILOGUE, NB)

        @block.gpsimd
        def _(pool):
            pool.memset(mhalf[:], -0.5).then_inc(pchain, 1)
            pool.wait_ge(pchain, 1)

            def rstd_of(b):
                pool.wait_ge(stats_ready, b + 1)
                settle(pool, passed)
                pool.tensor_scalar(ve[:], mv[:, :, 1], LN_EPS, None, ALU.add).then_inc(vchain, 1)
                pool.wait_ge(vchain, b + 1)
                pool.tensor_tensor(rstd[:], ve[:], mhalf[:], ALU.pow).then_inc(rstd_ready, 1)

            def context_low(b):
                pool.wait_ge(c_hi_done, b + 1)
                pool.tensor_tensor(c_lo[:], c_raw[:], c_hi[:].bitcast(F32), ALU.subtract).then_inc(c_split, 1)

            def pair_view(ten, odd):
                return ten[:].rearrange("p t (n two) -> p t n two", two=2)[:, :, :, odd]

            def rotate_first(b):
                pool.wait_ge(xn_ready, b + 1)
                pool.tensor_tensor(r1[:], pair_view(xn, 0), cos[:], ALU.mult).then_inc(rchain, 1)
                pool.tensor_tensor(r3[:], pair_view(xn, 1), sin[:], ALU.mult).then_inc(rchain, 1)
                pool.wait_ge(rchain, 2 * (b + 1))
                pool.tensor_tensor(pair_view(rope, 0), r1[:], r3[:], ALU.subtract).then_inc(roped, 1)

            def add_bo(b):
                pool.wait_ge(n_kept, b + 1)
                for t in range(TB):
                    xt = X[:, bass.ds(TB * b + t, 1), :].rearrange("p o n -> p (o n)")
                    made = pool.tensor_tensor(xt, xt, bo[:], ALU.add)
                made.then_inc(bo_added, 1)

            def bounce(G, slot, count, par, ready):
                pool.wait_ge(misc_read, ready)
                settle(pool, passed)
                pool.dma_start(m_scratch.rearrange("i c q -> c i q"), MT[:].bitcast(F32)).then_inc(m_out, 16)
                pool.wait_ge(m_out, 16 * count)
                settle(pool, passed)
                pool.dma_start(QS[AUG:AUG + 2, slot].rearrange("p j t -> p (j t)").bitcast(F32),
                               m_scratch.rearrange("i c q -> i (c q)")).then_inc(aug_in[par], 16)

            def add_output(G, b, go, ready):
                pool.wait_ge(misc_read, ready)
                dst = X[:, bass.ds(TB * b, TB), HG * DH * go:HG * DH * (go + 1)]
                pool.tensor_tensor(dst, dst, o_tmp[:], ALU.add).then_inc(o_added, 1)

            def second_stage(b):
                pool.wait_ge(ystats_ready, 2 * b)
                settle(pool, passed)
                pool.tensor_scalar(yve[:], ymv[:, :, 1], LN_EPS, None, ALU.add).then_inc(ychain, 1)
                pool.wait_ge(ychain, 2 * b - 1)
                pool.tensor_tensor(yrstd[:], yve[:], mhalf[:], ALU.pow).then_inc(yrstd_ready, 1)

            def apply_weights(b):
                pool.wait_ge(y_normed, b)
                lw = ln_w[:].unsqueeze(1).to_broadcast([P, TB, D])
                lb = ln_b[:].unsqueeze(1).to_broadcast([P, TB, D])
                pool.tensor_tensor(y[:], y[:], lw, ALU.mult).then_inc(ychain, 1)
                pool.wait_ge(ychain, 2 * b)
                pool.tensor_tensor(X[:, bass.ds(TB * (b - 1), TB), :], y[:], lb, ALU.add).then_inc(x1_done, 1)

            rstd_of(0)
            if layer1:
                pool.wait_ge(small_in, 128)
                rotate_first(0)
                add_bo(0)
            else:
                context_low(0)
            pool.memset(KS[:].bitcast(F32), 0.0).then_inc(zeroed, 1)
            pool.wait_ge(zeroed, 1)
            pool.memset(QS[:].bitcast(F32), 0.0).then_inc(zeroed, 1)
            pool.wait_ge(zeroed, 2)
            pool.memset(KS[AUG:AUG + 2].bitcast(F32), 1.0).then_inc(ones_set, 1)
            if layer1:
                pool.wait_ge(ones_set, 1)
                for m, pattern in ((identb, None), (mask_q, 1), (mask_k, -1)):
                    pool.memset(m[:], 0.0).then_inc(pchain, 1)
                pool.wait_ge(pchain, 4)
                pool.affine_select(out=identb[:], in_=identb[:], compare_op=ALU.not_equal, fill=1.0, base=0, pattern=[[-1, P]], channel_multiplier=1)
                pool.affine_select(out=mask_q[:], in_=mask_q[:], compare_op=ALU.is_ge, fill=-BIG, base=0, pattern=[[-1, P]], channel_multiplier=1)
                pool.affine_select(out=mask_k[:], in_=mask_k[:], compare_op=ALU.is_ge, fill=-BIG, base=0, pattern=[[1, P]], channel_multiplier=-1).then_inc(consts, 1)
            else:
                pool.wait_ge(ones_set, 1)
                pool.sem_inc(consts, 1)
            pool.wait_ge(consts, 1)
            bounce(0, 0, 1, 0, PROLOGUE.no("m"))

            def batch(b, order, first, last):
                for g in range(NG):
                    G = NG * b + g
                    if g == 0 and not last:
                        rstd_of(b + 1)
                    if not (last and g == NG - 1):
                        pool.wait_ge(aug_in[g % 2], 16 * (2 * b + g // 2 + 1))
                        bounce(G + 1, (g + 1) % NG, G + 2, (g + 1) % 2, order.no(f"m{g}"))
                    if not layer1 and not (first and g == 0):
                        add_output(G - 1, b if g else b - 1, (g - 1) % NG, order.no(f"OT{g}"))
                    if g == 0 and not last:
                        if layer1:
                            rotate_first(b + 1)
                            add_bo(b + 1)
                        else:
                            context_low(b + 1)
                    if layer1 and not first and g == 2:
                        second_stage(b)
                    if layer1 and not first and g == 3:
                        apply_weights(b)
            batches(pool, batch)
            if layer1:
                second_stage(NB)
                apply_weights(NB)
            else:
                add_output(NG * NB - 1, LASTB, NG - 1, EPILOGUE.no("OT"))


def moe_phase(nc, shared, prefix, ins, E, TOPK, renormalise, last_phase, out=None):
    X, ident, tg_all = shared["X"], shared["ident"], shared["tg"]
    NP = E // 2
    DVE_PAIRS = [p for p in range(NP) if p % 2 == 0 or p == NP - 1]
    ACT_PAIRS = [p for p in range(NP) if p not in DVE_PAIRS]
    ND, NA = len(DVE_PAIRS), len(ACT_PAIRS)
    NJ = 2 * NA
    UNITS = TB * NP
    PADS = 8 - TOPK
    RR = 4
    RD, RA, RM = 4, 2, 2
    with ExitStack() as stack:
        k = Kit(nc, prefix, stack)
        w_hi = k.sb("w_hi", [P, KC, E, D], F32R)
        w_lo = k.sb("w_lo", [P, KC, E, D], F32R)
        raw = k.sb("raw", [P, RR, KC, 2, D])
        rw_raw = k.sb("rw_raw", [P, KC, E])
        rw_hi = k.sb("rw_hi", [P, KC, E], F32R)
        rw_lo = k.sb("rw_lo", [P, KC, E], F32R)
        rb = k.sb("rb", [P, E])
        xn = k.sb("xn", [P, TB, D])
        x_hi = [k.sb(f"x_hi{i}", [P, KC, S], F32R) for i in range(2)]
        x_lo = [k.sb(f"x_lo{i}", [P, KC, S], F32R) for i in range(2)]
        gates = [k.sb(f"gates{i}", [P, TB, E]) for i in range(2)]
        addend = [k.sb(f"addend{i}", [P, TB]) for i in range(2)]
        acc_a = k.sb("acc_a", [P, 2, D])
        acc_b = k.sb("acc_b", [P, 2, D])
        scaled = k.sb("scaled", [P, NJ, D])
        stats = k.sb("stats", [P, TB, 6])
        mv = k.sb("mv", [P, TB, 2])
        ve = k.sb("ve", [P, TB])
        mhalf = k.sb("mhalf", [P, TB])
        rstd = k.sb("rstd", [P, TB])
        lg = k.sb("lg", [P, TB, E])
        ex = k.sb("ex", [P, TB, E])
        mx = k.sb("mx", [P, TB])
        sm = k.sb("sm", [P, TB])
        rs = k.sb("rs", [P, TB])
        probs = k.sb("probs", [P, TB, E + PADS])
        left = k.sb("left", [P, TB, E + PADS])
        top8 = k.sb("top8", [P, TB, 8])
        sel = k.sb("sel", [P, TB, E])
        if not renormalise:
            gT = [k.sb(f"gT{i}", [E, S]) for i in range(2)]
            x_last = k.sb("x_last", [P, NT, D])
            eb = k.sb("eb", [E, D])
            w2 = k.sb("w2", [P, D])
            b2 = k.sb("b2", [P, D])
            w2g = k.sb("w2g", [P, D])
            b2g = k.sb("b2g", [P, D])
            y = k.sb("y", [P, 2, D])
            fstats = k.sb("fstats", [P, 2, 6])
            fmv = k.sb("fmv", [P, 2, 2])
            fve = k.sb("fve", [P, 2])
            frstd = k.sb("frstd", [P, 2])
        bank_d = k.ps("bank_d", [P, RD, 512])
        bank_a = k.ps("bank_a", [P, RA, 512])
        bank_m = k.ps("bank_m", [P, RM, 512])

        passed = k.sem("passed")
        raw_in = [k.sem(f"raw_in{i}") for i in range(RR)]
        raw_hi_done, raw_lo_done = k.sem("raw_hi_done"), k.sem("raw_lo_done")
        small_in, router_split = k.sem("small_in"), k.sem("router_split")
        stats_ready, rstd_ready, xn_ready = k.sem("stats_ready"), k.sem("rstd_ready"), k.sem("xn_ready")
        misc_ready, router_taken, bias_added = k.sem("misc_ready"), k.sem("router_taken"), k.sem("bias_added")
        hi_done, x_split = k.sem("hi_done"), k.sem("x_split")
        shifted, exps, gates_ready = k.sem("shifted"), k.sem("exps"), k.sem("gates_ready")
        d_ready, d_free = k.sem("d_ready"), k.sem("d_free")
        a_ready = k.sem("a_ready")
        act_scaled, scaled_free = k.sem("act_scaled"), k.sem("scaled_free")
        dve_tile, pool_tile = k.sem("dve_tile"), k.sem("pool_tile")
        chain, pchain = k.sem("chain"), k.sem("pchain")
        gT_ready, pe_batch = k.sem("gT_ready"), k.sem("pe_batch")
        fstat_ready, frstd_ready, bias_first, normed, ychain, y_ready = (
            k.sem("fstat_ready"), k.sem("frstd_ready"), k.sem("bias_first"), k.sem("normed"), k.sem("ychain"), k.sem("y_ready"))
        x_last_in = k.sem("x_last_in")
        y_stored = [k.sem(f"y_stored{i}") for i in range(2)]

        if NP == 8:
            TASKS = [("xT0", 8), ("xT1", 11), ("router", 17)]
        else:
            TASKS = [("xT0", 1), ("xT1", 2), ("router", 5), ("gT", 11), ("eb0", 13), ("eb1", 15)]
        if renormalise:
            TASKS = TASKS[:3]
        NM = len(TASKS)

        def m_base(b):
            return NM * b

        def slot(i, half):
            return (NM * half + i) % RM

        def halves(eng, body):
            if not renormalise:
                for half in range(2):
                    body(half, half, True)
            with eng.Fori(0 if renormalise else 1, NB // 2 - 1) as r:
                for half in range(2):
                    body(2 * r + half, half, True)
            for half in range(2):
                body(NB - 2 + half, half, half == 0)

        def back(b, t, n):
            return (b, t - n) if t >= n else (b - 1, t - n + TB)

        block = stack.enter_context(nc.Block())

        @block.sync
        def _(sp):
            sp.dma_start(rw_raw[:], ins["router"].rearrange("(c p) e -> p c e", p=P)).then_inc(small_in, 16)
            sp.dma_start(rb[:], ins["router_b"].partition_broadcast(P)).then_inc(small_in, 16)
            if not renormalise:
                sp.dma_start(eb[:], ins["expert_b"]).then_inc(small_in, 16)
                sp.dma_start(w2[:], ins["ln_w"].partition_broadcast(P)).then_inc(small_in, 16)
                sp.dma_start(b2[:], ins["ln_b"].partition_broadcast(P)).then_inc(small_in, 16)
            for q in range(NP):
                if q >= RR:
                    sp.wait_ge(raw_lo_done, q - RR + 1)
                for e in range(2):
                    sp.dma_start(raw[:, q % RR, :, e, :],
                                 ins["expert"][2 * q + e].rearrange("(c p) n -> p c n", p=P)).then_inc(raw_in[q % RR], 16)
            if last_phase:
                sp.dma_start(x_last[:], ins["x_mid"].rearrange("t p n -> p t n")).then_inc(x_last_in, 16)

                def store(b, half, _):
                    for t in range(TB):
                        sp.wait_ge(y_ready, TB * b + t + 1)
                        settle(sp, passed)
                        sp.dma_start(out[bass.ds(TB * b + t, 1), :, :].rearrange("o p n -> p (o n)"), y[:, t % 2, :]).then_inc(y_stored[t % 2], 16)
                halves(sp, store)
                for i in range(2):
                    sp.wait_ge(y_stored[i], 16 * (NT // 2) + 16)

        @block.tensor
        def _(pe):
            def x_transposes(c, s):
                for t in range(TB):
                    src = xn[:, t, c * P:(c + 1) * P]
                    made = pe.transpose(bank_m[:, s, t * P:(t + 1) * P], src, ident[:])
                made.then_inc(misc_ready, 1)

            def router(s, par):
                for t in range(TB):
                    made = three_pass(pe, bank_m[:, s, t * E:(t + 1) * E],
                                      [(x_hi[par][:, c, t * P:(t + 1) * P], x_lo[par][:, c, t * P:(t + 1) * P]) for c in range(KC)],
                                      [(rw_hi[:, c, :], rw_lo[:, c, :]) for c in range(KC)])
                made.then_inc(misc_ready, 1)

            def prepare(b, par, first=False):
                def xT0():
                    pe.wait_ge(xn_ready, b + 1)
                    if not renormalise and not first:
                        pe.wait_ge(bias_added, 2 * b - 1)
                    x_transposes(0, slot(0, par))

                def xT1():
                    if not first:
                        pe.wait_ge(*((router_taken, b) if renormalise else (bias_added, 2 * b)))
                    x_transposes(1, slot(1, par))

                def logits():
                    pe.wait_ge(x_split, 2 * b + 2)
                    if first:
                        pe.wait_ge(router_split, 1)
                    router(slot(2, par), par)

                def gate_transposes():
                    pe.wait_ge(gates_ready, b + 1)
                    for t in range(TB):
                        made = pe.transpose(bank_m[0:E, slot(3, par), t * P:(t + 1) * P], gates[par][:, t, :], ident[:])
                    made.then_inc(misc_ready, 1)

                def bias_products(i):
                    pe.wait_ge(gT_ready, b + 1)
                    for j in range(2):
                        t = 2 * i + j
                        made = pe.matmul(bank_m[:, slot(4 + i, par), j * D:(j + 1) * D],
                                         gT[par][:, t * P:(t + 1) * P], eb[:], start=True, stop=True)
                    made.then_inc(misc_ready, 1)
                return [xT0, xT1, logits, gate_transposes, lambda: bias_products(0), lambda: bias_products(1)][:NM]

            for f in prepare(0, 0, True):
                f()
            pe.wait_ge(raw_lo_done, NP)

            def batch(b, half, more):
                par = half
                tasks = dict(zip([u for _, u in TASKS], prepare(b + 1, 1 - par))) if more else {}
                for t in range(TB):
                    x_t = [(x_hi[par][:, c, t * P:(t + 1) * P], x_lo[par][:, c, t * P:(t + 1) * P]) for c in range(KC)]
                    for p in range(NP):
                        w_p = [(w_hi[:, c, 2 * p:2 * p + 2, :].rearrange("p e n -> p (e n)"), w_lo[:, c, 2 * p:2 * p + 2, :].rearrange("p e n -> p (e n)")) for c in range(KC)]
                        if p in DVE_PAIRS:
                            i = ND * t + DVE_PAIRS.index(p)
                            pe.wait_ge(d_free, ND * TB * b + i + 1)
                            three_pass(pe, bank_d[:, (ND * TB * half + i) % RD, :], x_t, w_p).then_inc(d_ready, 1)
                        else:
                            i = NA * t + ACT_PAIRS.index(p)
                            pe.wait_ge(act_scaled, 2 * (NA * TB * b + i) + 2)
                            made = three_pass(pe, bank_a[:, (NA * TB * half + i) % RA, :], x_t, w_p)
                            made.then_inc(a_ready, 1)
                        f = tasks.get(NP * t + p)
                        if f:
                            f()
            halves(pe, batch)

        @block.vector
        def _(dve):
            link = Tally(dve, chain)

            def weights():
                dve.sem_inc(d_free, RD)
                link.done(dve.memset(probs[:, :, E:], BIG))
                dve.wait_ge(small_in, 16 * (2 if renormalise else 5))
                link.done(dve.tensor_copy(rw_hi[:], rw_raw[:]))
                link.wait()
                dve.tensor_tensor(rw_lo[:], rw_raw[:], rw_hi[:].bitcast(F32), ALU.subtract).then_inc(router_split, 1)
                if not renormalise:
                    link.done(dve.tensor_scalar(w2g[:], w2[:], tg_all[:, 0:1], None, ALU.mult))
                    link.done(dve.tensor_scalar(b2g[:], b2[:], tg_all[:, 0:1], None, ALU.mult))

            def experts():
                for q in range(NP):
                    dve.wait_ge(raw_hi_done, q + 1)
                    dve.tensor_tensor(w_lo[:, :, 2 * q:2 * q + 2, :], raw[:, q % RR], w_hi[:, :, 2 * q:2 * q + 2, :].bitcast(F32),
                                      ALU.subtract).then_inc(raw_lo_done, 1)

            def tile_of(ten, b, t):
                return ten[:, bass.ds(TB * b + t, 1), :].rearrange("p o n -> p (o n)")

            def norm_stats(b, link):
                if not renormalise:
                    return
                for t in range(TB):
                    link.done(dve.bn_stats(stats[:, t, :], tile_of(X, b, t)))
                link.wait()
                settle(dve, passed)
                for t in range(TB):
                    made = dve.bn_aggr(mv[:, t, :], stats[:, t, :])
                made.then_inc(stats_ready, 1)

            def norm_apply(b):
                if renormalise:
                    dve.wait_ge(rstd_ready, b + 1)
                for t in range(TB):
                    if renormalise:
                        made = dve.tensor_scalar(xn[:, t, :], tile_of(X, b, t), mv[:, t, 0:1], rstd[:, t:t + 1], ALU.subtract, ALU.mult)
                if renormalise:
                    made.then_inc(xn_ready, 1)

            def split_low(b, c, s, par):
                dve.wait_ge(hi_done, 2 * b + c + 1)
                made = dve.tensor_tensor(x_lo[par][:, c, :], bank_m[:, s, :], x_hi[par][:, c, :].bitcast(F32), ALU.subtract)
                made.then_inc(x_split, 1)

            def wide(ap):
                return ap.unsqueeze(2).to_broadcast([P, TB, E])

            def gates_one(b, number, s, link):
                dve.wait_ge(misc_ready, number + 1)
                made = dve.tensor_tensor(lg[:], bank_m[:, s, 0:TB * E].rearrange("p (t e) -> p t e", e=E),
                                         rb[:].unsqueeze(1).to_broadcast([P, TB, E]), ALU.add)
                made.then_inc(router_taken, 1)
                dve.wait_ge(router_taken, b + 1)
                link.done(dve.tensor_reduce(mx[:], lg[:], axis=AX.X, op=ALU.max))
                link.wait()
                dve.tensor_tensor(lg[:], lg[:], wide(mx[:]), ALU.subtract).then_inc(shifted, 1)

            def gates_two(b, par, link):
                dve.wait_ge(exps, b + 1)
                link.done(dve.tensor_reduce(sm[:], ex[:], axis=AX.X, op=ALU.add))
                link.wait()
                link.done(dve.reciprocal(rs[:], sm[:]))
                link.wait()
                link.done(dve.tensor_tensor(probs[:, :, 0:E], ex[:], wide(rs[:]), ALU.mult))
                link.wait()
                settle(dve, passed)
                for t in range(TB):
                    link.done(dve.max(top8[:, t, :], probs[:, t, :]))
                link.wait()
                settle(dve, passed)
                for t in range(TB):
                    link.done(dve.match_replace(left[:, t, :], top8[:, t, :], probs[:, t, :], -1.0))
                link.wait()
                g = gates[par]
                made = dve.scalar_tensor_tensor(sel[:] if renormalise else g[:], left[:, :, 0:E], 0.0, probs[:, :, 0:E], ALU.is_lt, ALU.mult)
                if not renormalise:
                    made.then_inc(gates_ready, 1)
                    return
                link.done(made)
                link.wait()
                link.done(dve.tensor_reduce(sm[:], sel[:], axis=AX.X, op=ALU.add))
                link.wait()
                link.done(dve.tensor_scalar(sm[:], sm[:], 1e-10, None, ALU.add))
                link.wait()
                link.done(dve.reciprocal(rs[:], sm[:]))
                link.wait()
                link.done(dve.tensor_tensor(sel[:], sel[:], wide(rs[:]), ALU.mult))
                link.wait()
                link.done(dve.tensor_reduce(sm[:], sel[:], axis=AX.X, op=ALU.add))
                link.wait()
                link.done(dve.tensor_scalar(mx[:], sm[:], 1e-10, None, ALU.max))
                link.done(dve.tensor_scalar(addend[par][:], sm[:], tg_all[:, 0:1], 1e-10, ALU.mult, ALU.mult))
                link.wait()
                link.done(dve.reciprocal(rs[:], mx[:]))
                link.wait()
                link.done(dve.tensor_scalar(rs[:], rs[:], tg_all[:, 0:1], None, ALU.mult))
                link.wait()
                dve.tensor_tensor(g[:], sel[:], wide(rs[:]), ALU.mult).then_inc(gates_ready, 1)

            def bias_add(b, i, par):
                dve.wait_ge(misc_ready, m_base(b) + 4 + i + 1)
                for j in range(2):
                    dst = tile_of(X, b, 2 * i + j)
                    made = dve.tensor_tensor(dst, bank_m[:, slot(4 + i, par), j * D:(j + 1) * D], dst, ALU.add)
                    made.then_inc(*((bias_added, 1) if j else (bias_first, 1)))

            def finish_stats(b, t, link):
                dve.wait_ge(pool_tile, 2 + TB * b + t + 1)
                settle(dve, passed)
                link.done(dve.bn_stats(fstats[:, t % 2, :], tile_of(X, b, t)))
                link.wait()
                settle(dve, passed)
                dve.bn_aggr(fmv[:, t % 2, :], fstats[:, t % 2, :]).then_inc(fstat_ready, 1)

            def finish_tile(b, t, link):
                dve.wait_ge(frstd_ready, TB * b + t + 1)
                dve.wait_ge(y_stored[t % 2], 16 * (TB // 2 * b + t // 2) + 16)
                dve.tensor_scalar(y[:, t % 2, :], tile_of(X, b, t), fmv[:, t % 2, 0:1], frstd[:, t % 2:t % 2 + 1],
                                  ALU.subtract, ALU.mult).then_inc(normed, 1)

            weights()
            norm_stats(0, link)
            norm_apply(0)
            experts()
            split_low(0, 0, 0, 0)
            split_low(0, 1, 1, 0)
            gates_one(0, 2, 0, link)
            gates_two(0, 0, link)
            if not renormalise:
                bias_add(0, 0, 0)
                bias_add(0, 1, 0)
            BASE = link.n
            LEN = shared["lens"].get(prefix, 0)

            def batch(b, half, more):
                par = half
                first = isinstance(b, int) and b == 0
                late = 0 if renormalise or first else 1
                link = Tally(dve, chain, BASE + LEN * b - late)
                jobs = {}
                if more:
                    nxt = 1 - par
                    at = (1, 5, 9, 12, 18, 22) if NP == 8 else (0, 1, 2, 3, 6, 8)
                    jobs[at[0]] = [lambda: norm_stats(b + 1, link)]
                    jobs[at[1]] = [lambda: norm_apply(b + 1)]
                    jobs[at[2]] = [lambda: split_low(b + 1, 0, slot(0, nxt), nxt)]
                    jobs[at[3]] = [lambda: split_low(b + 1, 1, slot(1, nxt), nxt)]
                    jobs[at[4]] = [lambda: gates_one(b + 1, m_base(b + 1) + 2, slot(2, nxt), link)]
                    jobs[at[5]] = [lambda: gates_two(b + 1, nxt, link)]
                    if not renormalise:
                        jobs[13] = [lambda: bias_add(b + 1, 0, nxt)]
                        jobs[15] = [lambda: bias_add(b + 1, 1, nxt)]
                g = gates[par]
                dve.wait_ge(gates_ready, b + 1)
                if not renormalise:
                    dve.wait_ge(bias_added, 2 * b + 2)
                for t in range(TB):
                    xt = tile_of(X, b, t)
                    at_ = acc_a[:, t % 2, :]
                    for p in range(NP):
                        if p in DVE_PAIRS:
                            i = ND * t + DVE_PAIRS.index(p)
                            bank = bank_d[:, (ND * TB * half + i) % RD, :]
                            dve.wait_ge(d_ready, ND * TB * b + i + 1)
                            link.wait()
                            link.done(dve.scalar_tensor_tensor(xt, bank[:, 0:D], g[:, t, 2 * p:2 * p + 1], xt, ALU.mult, ALU.add))
                            dve.wait_ge(d_free, RD + ND * TB * b + i)
                            if p == DVE_PAIRS[0]:
                                made = dve.tensor_scalar(at_, bank[:, D:2 * D], g[:, t, 2 * p + 1:2 * p + 2], None, ALU.mult)
                            else:
                                made = dve.scalar_tensor_tensor(at_, bank[:, D:2 * D], g[:, t, 2 * p + 1:2 * p + 2], at_, ALU.mult, ALU.add)
                            made.then_inc(d_free, 1)
                        for f in jobs.get(NP * t + p, []):
                            f()
                    link.wait()
                    dve.wait_ge(d_free, RD + ND * (TB * b + t + 1))
                    dve.tensor_tensor(xt, xt, at_, ALU.add).then_inc(dve_tile, 1)
                    if not renormalise and not (first and t == 0):
                        finish_stats(*back(b, t, 1), link)
                        if not (first and t == 1):
                            finish_tile(*back(b, t, 2), link)
                if not renormalise and not more and half == 1:
                    finish_tile(b, TB - 2, link)
                    finish_stats(b, TB - 1, link)
                    finish_tile(b, TB - 1, link)
                if more:
                    assert link.n == LEN - (1 if first and not renormalise else 0), f"{prefix} chain {link.n}"
            halves(dve, batch)

        @block.scalar
        def _(act):
            act.sem_inc(act_scaled, 2 * RA)
            for q in range(NP):
                act.wait_ge(raw_in[q % RR], 32 * (q // RR + 1))
                act.activation(w_hi[:, :, 2 * q:2 * q + 2, :].rearrange("p c e n -> p c (e n)"), raw[:, q % RR].rearrange("p c e n -> p c (e n)"), ACT.Copy).then_inc(raw_hi_done, 1)

            def split_high(number, c, s, par):
                act.wait_ge(misc_ready, number + 1)
                act.activation(x_hi[par][:, c, :], bank_m[:, s, :], ACT.Copy).then_inc(hi_done, 1)

            def copy_x1(b):
                for t in range(TB):
                    made = act.activation(xn[:, t, :], X[:, bass.ds(TB * b + t, 1), :].rearrange("p o n -> p (o n)"), ACT.Copy)
                made.then_inc(xn_ready, 1)

            def gT_copy(b, par):
                act.wait_ge(misc_ready, m_base(b) + 3 + 1)
                act.activation(gT[par][:], bank_m[0:E, slot(3, par), :], ACT.Copy).then_inc(gT_ready, 1)

            def exponentials(b):
                act.wait_ge(shifted, b + 1)
                act.activation(ex[:], lg[:], ACT.Exp).then_inc(exps, 1)

            if not renormalise:
                copy_x1(0)
            split_high(0, 0, 0, 0)
            split_high(1, 1, 1, 0)
            exponentials(0)
            if not renormalise:
                gT_copy(0, 0)

            def batch(b, half, more):
                par = half
                jobs = {}
                if more:
                    nxt, no = 1 - par, m_base(b + 1)
                    at = (9, 12, 19) if NP == 8 else (2, 3, 6)
                    jobs[at[0]] = [lambda: split_high(no, 0, slot(0, nxt), nxt)]
                    jobs[at[1]] = [lambda: split_high(no + 1, 1, slot(1, nxt), nxt)]
                    jobs[at[2]] = [lambda: exponentials(b + 1)]
                    if not renormalise:
                        jobs[0] = [lambda: copy_x1(b + 1)]
                        jobs[12] = [lambda: gT_copy(b + 1, nxt)]
                g = gates[par]
                act.wait_ge(gates_ready, b + 1)
                for t in range(TB):
                    for p in range(NP):
                        if p in ACT_PAIRS:
                            i = NA * t + ACT_PAIRS.index(p)
                            bank = bank_a[:, (NA * TB * half + i) % RA, :]
                            act.wait_ge(a_ready, NA * TB * b + i + 1)
                            for e in range(2):
                                j = 2 * ACT_PAIRS.index(p) + e
                                gate = g[:, t, 2 * p + e:2 * p + e + 1]
                                if j == 0:
                                    act.wait_ge(pool_tile, TB * b + t + 1)
                                    if renormalise:
                                        made = act.activation(acc_b[:, t % 2, :], bank[:, 0:D], ACT.Identity, scale=gate, bias=addend[par][:, t:t + 1])
                                    else:
                                        made = act.activation(acc_b[:, t % 2, :], bank[:, 0:D], ACT.Copy, scale=gate)
                                else:
                                    act.wait_ge(scaled_free, (NJ - 1) * (TB * b + t) + j)
                                    made = act.activation(scaled[:, j, :], bank[:, e * D:(e + 1) * D], ACT.Copy, scale=gate)
                                made.then_inc(act_scaled, 1)
                        for f in jobs.get(NP * t + p, []):
                            f()
            halves(act, batch)

        @block.gpsimd
        def _(pool):
            pool.sem_inc(pool_tile, 2)
            pool.sem_inc(scaled_free, NJ - 1)
            if last_phase:
                for i in range(2):
                    pool.sem_inc(y_stored[i], 16)
            pool.memset(mhalf[:], -0.5).then_inc(pchain, 1)
            pool.wait_ge(pchain, 1)

            def rstd_of(b):
                pool.wait_ge(stats_ready, b + 1)
                settle(pool, passed)
                pool.tensor_scalar(ve[:], mv[:, :, 1], LN_EPS, None, ALU.add).then_inc(pchain, 1)
                pool.wait_ge(pchain, b + 2)
                pool.tensor_tensor(rstd[:], ve[:], mhalf[:], ALU.pow).then_inc(rstd_ready, 1)

            def frstd_of(b, t):
                pool.wait_ge(fstat_ready, TB * b + t + 1)
                settle(pool, passed)
                pool.tensor_scalar(fve[:, t % 2:t % 2 + 1], fmv[:, t % 2, 1:2], LN_EPS, None, ALU.add).then_inc(pchain, 1)
                pool.wait_ge(pchain, TB * b + t + 2)
                pool.tensor_tensor(frstd[:, t % 2:t % 2 + 1], fve[:, t % 2:t % 2 + 1], mhalf[:, 0:1], ALU.pow).then_inc(frstd_ready, 1)

            def finish_tile(b, t):
                xt = x_last[:, bass.ds(TB * b + t, 1), :].rearrange("p o n -> p (o n)")
                yt = y[:, t % 2, :]
                pool.wait_ge(normed, TB * b + t + 1)
                for i, (other, op) in enumerate(((w2g[:], ALU.mult), (b2g[:], ALU.add), (xt, ALU.add))):
                    made = pool.tensor_tensor(yt, yt, other, op)
                    if i < 2:
                        made.then_inc(ychain, 1)
                        pool.wait_ge(ychain, 2 * (TB * b + t) + i + 1)
                made.then_inc(y_ready, 1)

            if renormalise:
                rstd_of(0)
            else:
                pool.wait_ge(x_last_in, 16)

            def batch(b, half, more):
                first = isinstance(b, int) and b == 0
                if more and renormalise:
                    rstd_of(b + 1)
                for t in range(TB):
                    acc = acc_b[:, t % 2, :]
                    for j in range(1, NJ):
                        pool.wait_ge(act_scaled, 2 * RA + NJ * (TB * b + t) + j + 1)
                        pool.wait_ge(scaled_free, (NJ - 1) * (TB * b + t + 1) + j - 1)
                        pool.tensor_tensor(acc, acc, scaled[:, j, :], ALU.add).then_inc(scaled_free, 1)
                    pool.wait_ge(dve_tile, TB * b + t + 1)
                    pool.wait_ge(scaled_free, (NJ - 1) * (TB * b + t + 2))
                    xt = X[:, bass.ds(TB * b + t, 1), :].rearrange("p o n -> p (o n)")
                    pool.tensor_tensor(xt, xt, acc, ALU.add).then_inc(pool_tile, 1)
                    if not renormalise:
                        if not (first and t == 0):
                            frstd_of(*back(b, t, 1))
                            if not (first and t == 1):
                                finish_tile(*back(b, t, 2))
                if not renormalise and not more and half == 1:
                    finish_tile(b, TB - 2)
                    frstd_of(b, TB - 1)
                    finish_tile(b, TB - 1)
            halves(pool, batch)


def xattn_phase(nc, shared, prefix, ins, x_mid):
    X, ident, tg = shared["X"], shared["ident"], shared["tg"]
    SCALE = D ** -0.5
    MASKED = -1e9 / SCALE
    NPREP = 8
    SLOTS = {1: (("x0", "x1"), ("k0",)), 2: (("k1", "q0"), ("q1",)), 3: (("v0",), ("v1",))}
    TASKS = [n for t in (1, 2, 3) for part in SLOTS[t] for n in part]
    with ExitStack() as stack:
        k = Kit(nc, prefix, stack)
        sb, sem = k.sb, k.sem
        w_raw = {n: sb(f"w{n}_raw", [P, KC, D]) for n in "kqv"}
        w_hi = {n: sb(f"w{n}_hi", [P, KC, D], F32R) for n in "kqv"}
        w_lo = {n: sb(f"w{n}_lo", [P, KC, D], F32R) for n in "kqv"}
        bias = {n: sb(f"b{n}", [P, KC]) for n in "kq"}
        bv = sb("bv", [P, D])
        c_raw = sb("c_raw", [P, KC, S])
        c_hi, c_lo = sb("c_hi", [P, KC, S], F32R), sb("c_lo", [P, KC, S], F32R)
        xn = sb("xn", [P, TB, D])
        x_hi, x_lo = sb("x_hi", [P, KC, S], F32R), sb("x_lo", [P, KC, S], F32R)
        parts = {n: [(sb(f"{n}_hi{i}", [P, KC, S], F32R), sb(f"{n}_lo{i}", [P, KC, S], F32R)) for i in range(2)] for n in "kq"}
        v_parts = [(sb(f"v_hi{i}", [P, TB, D], F32R), sb(f"v_lo{i}", [P, TB, D], F32R)) for i in range(2)]
        v_sum = [sb(f"v_sum{i}", [P, 2, D]) for i in range(2)]
        mask = [sb(f"mask{i}", [P, TB, S], U8) for i in range(2)]
        masked = sb("masked", [P, S])
        nmax, nbias = sb("nmax", [P, 2]), sb("nbias", [P, 2])
        sums, rec = sb("sums", [P, 4]), sb("rec", [P, 2])
        PM = sb("PM", [P, 2, S])
        pt_hi = [sb(f"pt_hi{i}", [P, S], F32R) for i in range(2)]
        pt_lo = [sb(f"pt_lo{i}", [P, S], F32R) for i in range(2)]
        stats, mv = sb("stats", [P, TB, 6]), sb("mv", [P, TB, 2])
        ve, mhalf, rstd = sb("ve", [P, TB]), sb("mhalf", [P, TB]), sb("rstd", [P, TB])
        misc, sc = k.ps("misc", [P, 2, S]), k.ps("sc", [P, 2, S])
        pt, yb = k.ps("pt", [P, 2, S]), k.ps("yb", [P, 2, S])

        passed = sem("passed")
        w_in, w_hi_done, w_split, small_in, consts = (sem(n) for n in ("w_in", "w_hi_done", "w_split", "small_in", "consts"))
        c_in, c_hi_done, c_split = sem("c_in"), sem("c_hi_done"), sem("c_split")
        mask_in = [sem(f"mask_in{i}") for i in range(2)]
        stats_made, stats_ready, ve_made, rstd_ready, xn_ready = (sem(n) for n in ("stats_made", "stats_ready", "ve_made", "rstd_ready", "xn_ready"))
        misc_ready, hi_done, misc_read = sem("misc_ready"), sem("hi_done"), sem("misc_read")
        v_hi_done, v_split = sem("v_hi_done"), sem("v_split")
        s_ready, s_masked, max_done, bias_ready, exp_done = (sem(n) for n in ("s_ready", "s_masked", "max_done", "bias_ready", "exp_done"))
        pt_ready, pt_hi_done, pt_split = sem("pt_ready"), sem("pt_hi_done"), sem("pt_split")
        y_ready, rec_made, x_done, x_stored = sem("y_ready"), sem("rec_made"), sem("x_done"), sem("x_stored")

        def number(b, name):
            return NPREP * b + TASKS.index(name) + 1

        def hi_number(b, name):
            return 6 * b + TASKS.index(name) + 1

        def ge(eng, s, value):
            if not (isinstance(value, int) and value <= 0):
                eng.wait_ge(s, value)

        def batches(eng, body):
            body(0, 0, False)
            with eng.Fori(0, (NB - 2) // 2) as i:
                body(2 * i + 1, 1, False)
                body(2 * i + 2, 0, False)
            body(NB - 1, (NB - 1) % 2, True)

        def xtile(b, t):
            return X[:, bass.ds(TB * b + t, 1), :].rearrange("p o n -> p (o n)")

        block = stack.enter_context(nc.Block())

        @block.sync
        def _(sp):
            for i, n in enumerate("kqv"):
                sp.dma_start(w_raw[n][:], ins["w" + n].rearrange("(c p) n -> p c n", p=P)).then_inc(w_in, 16)
                if i == 0:
                    sp.dma_start(c_raw[:], ins["ctxT"][0].rearrange("(c p) t -> p c t", p=P)).then_inc(c_in, 16)
            sp.dma_start(bias["q"][:], ins["bq"]).then_inc(small_in, 16)
            sp.dma_start(bias["k"][:], ins["bk"]).then_inc(small_in, 16)
            sp.dma_start(bv[:], ins["bv"].partition_broadcast(P)).then_inc(small_in, 16)

            def load_mask(b, par):
                ge(sp, s_masked, TB * (b - 1))
                settle(sp, passed)
                sp.dma_start(mask[par][:], ins["mask"][bass.ds(b, 1)].rearrange("o (t p) j -> p (o t) j", p=P)).then_inc(mask_in[par], 16)

            def load_ctx(b):
                sp.wait_ge(c_split, b)
                settle(sp, passed)
                sp.dma_start(c_raw[:], ins["ctxT"][bass.ds(b, 1)].rearrange("o (c p) t -> p (o c) t", p=P)).then_inc(c_in, 16)

            def store_x(b):
                sp.wait_ge(x_done, TB * (b + 1))
                settle(sp, passed)
                sp.dma_start(x_mid[bass.ds(TB * b, TB)].rearrange("t p n -> p t n"), X[:, bass.ds(TB * b, TB), :]).then_inc(x_stored, 16)

            load_mask(0, 0)
            load_ctx(1)
            load_mask(1, 1)
            with sp.Fori(0, (NB - 2) // 2) as i:
                for par in range(2):
                    b = 2 * i + 2 + par
                    load_ctx(b)
                    load_mask(b, par)
                    store_x(b - 2)
            store_x(NB - 2)
            store_x(NB - 1)
            sp.wait_ge(x_stored, 16 * NB)

        @block.tensor
        def _(pe):
            def pairs(hi, lo, cut):
                return [(hi[:, c, cut], lo[:, c, cut]) for c in range(KC)]

            def prepare(name, b, par):
                kind, h = name[0], int(name[1])
                bank = TASKS.index(name) % 2
                ge(pe, misc_read, number(b, name) - 2)
                if kind == "x":
                    pe.wait_ge(xn_ready, b + 1)
                    for t in range(TB):
                        made = pe.transpose(misc[:, bank, t * P:(t + 1) * P], xn[:, t, h * P:(h + 1) * P], ident[:])
                elif kind == "v":
                    for j in range(2):
                        t = 2 * h + j
                        made = three_pass(pe, misc[:, bank, j * D:(j + 1) * D], pairs(c_hi, c_lo, slice(t * P, (t + 1) * P)),
                                          pairs(w_hi["v"], w_lo["v"], slice(0, D)))
                else:
                    if kind == "k":
                        pe.wait_ge(c_split, b + 1)
                    if name == "q0":
                        pe.wait_ge(misc_read, number(b, "x1"))
                    hi, lo = (c_hi, c_lo) if kind == "k" else (x_hi, x_lo)
                    made = three_pass(pe, misc[:, bank, :], pairs(w_hi[kind], w_lo[kind], slice(h * P, (h + 1) * P)), pairs(hi, lo, slice(0, S)))
                made.then_inc(misc_ready, 1)

            def scores(G, t, par):
                ge(pe, exp_done, G - 1)
                q, kk = parts["q"][par], parts["k"][par]
                three_pass(pe, sc[:, t % 2, :], pairs(*q, slice(t * P, (t + 1) * P)), pairs(*kk, slice(0, S))).then_inc(s_ready, 1)

            def transposes(G, t):
                pe.wait_ge(exp_done, G + 1)
                ge(pe, pt_split, G - 1)
                for c in range(TB):
                    made = pe.transpose(pt[:, t % 2, c * P:(c + 1) * P], PM[:, t % 2, c * P:(c + 1) * P], ident[:])
                made.then_inc(pt_ready, 1)

            def values(G, b, t, par):
                pe.wait_ge(pt_split, G + 1)
                if t == 0:
                    pe.wait_ge(v_split, 2 * (b + 1))
                ge(pe, x_done, G - 1)
                three_pass(pe, yb[:, t % 2, 0:D], [(pt_hi[t % 2][:, c * P:(c + 1) * P], pt_lo[t % 2][:, c * P:(c + 1) * P]) for c in range(TB)],
                           [(v_parts[par][0][:, c, :], v_parts[par][1][:, c, :]) for c in range(TB)]).then_inc(y_ready, 1)

            pe.wait_ge(w_split, 3)
            for name in TASKS:
                prepare(name, 0, 0)

            def batch(b, par, last):
                first = isinstance(b, int) and b == 0
                pe.wait_ge(misc_read, number(b, "q1"))
                for t in range(TB):
                    G = TB * b + t
                    scores(G, t, par)
                    one, two = SLOTS.get(t, ((), ())) if not last else ((), ())
                    for name in one:
                        prepare(name, b + 1, 1 - par)
                    if not (first and t == 0):
                        transposes(G - 1, (t - 1) % TB)
                    for name in two:
                        prepare(name, b + 1, 1 - par)
                    if not (first and t < 2):
                        back = t < 2
                        values(G - 2, b - 1 if back else b, (t - 2) % TB, 1 - par if back else par)
            batches(pe, batch)
            transposes(TB * NB - 1, TB - 1)
            values(TB * NB - 2, NB - 1, TB - 2, (NB - 1) % 2)
            values(TB * NB - 1, NB - 1, TB - 1, (NB - 1) % 2)

        @block.vector
        def _(dve):
            def norm_stats(b):
                for t in range(TB):
                    dve.bn_stats(stats[:, t, :], xtile(b, t)).then_inc(stats_made, 1)
                dve.wait_ge(stats_made, TB * (b + 1))
                settle(dve, passed)
                for t in range(TB):
                    made = dve.bn_aggr(mv[:, t, :], stats[:, t, :])
                made.then_inc(stats_ready, 1)

            def norm_apply(b):
                dve.wait_ge(rstd_ready, b + 1)
                ge(dve, misc_ready, number(b - 1, "x1"))
                for t in range(TB):
                    made = dve.tensor_scalar(xn[:, t, :], xtile(b, t), mv[:, t, 0:1], rstd[:, t:t + 1], ALU.subtract, ALU.mult)
                made.then_inc(xn_ready, 1)

            def low_part(name, b, par):
                kind, h = name[0], int(name[1])
                bank = TASKS.index(name) % 2
                if kind == "v":
                    dve.wait_ge(misc_ready, number(b, name))
                    ge(dve, v_split, 2 * (b - 1) + h + 1)
                    dve.tensor_tensor(v_sum[h][:], misc[:, bank, :].rearrange("p (t n) -> p t n", t=2),
                                      bv[:].unsqueeze(1).to_broadcast([P, 2, D]), ALU.add).then_inc(misc_read, 1)
                    return
                dve.wait_ge(hi_done, hi_number(b, name))
                if kind == "x":
                    made = dve.tensor_tensor(x_lo[:, h, :], misc[:, bank, :], x_hi[:, h, :].bitcast(F32), ALU.subtract)
                else:
                    hi, lo = parts[kind][par]
                    made = dve.scalar_tensor_tensor(lo[:, h, :], misc[:, bank, :], bias[kind][:, h:h + 1], hi[:, h, :].bitcast(F32), ALU.add, ALU.subtract)
                made.then_inc(misc_read, 1)

            def mask_and_max(G, t, par, b):
                if t == 0:
                    dve.wait_ge(mask_in[par], 16 * count_of(b, par))
                dve.wait_ge(s_ready, G + 1)
                settle(dve, passed)
                dve.copy_predicated(sc[:, t % 2, :], mask[par][:, t, :], masked[:]).then_inc(s_masked, 1)
                dve.wait_ge(s_masked, G + 1)
                dve.tensor_reduce(nmax[:, t % 2:t % 2 + 1], sc[:, t % 2, :], axis=AX.X, op=ALU.max, negate=True).then_inc(max_done, 1)
                dve.wait_ge(max_done, G + 1)
                ge(dve, exp_done, G - 1)
                dve.tensor_scalar(nbias[:, t % 2:t % 2 + 1], nmax[:, t % 2:t % 2 + 1], SCALE, None, ALU.mult).then_inc(bias_ready, 1)

            def count_of(b, par):
                if isinstance(b, int):
                    return b // 2 + 1
                return b_pair[0] + 2 - par

            def pt_low(G, t):
                dve.wait_ge(pt_hi_done, G + 1)
                dve.tensor_tensor(pt_lo[t % 2][:], pt[:, t % 2, :], pt_hi[t % 2][:].bitcast(F32), ALU.subtract).then_inc(pt_split, 1)

            def output(G, b, t):
                r = rec[:, t % 2:t % 2 + 1]
                dve.reciprocal(r, sums[:, t:t + 1]).then_inc(rec_made, 1)
                dve.wait_ge(rec_made, 2 * G + 1)
                dve.tensor_scalar(r, r, tg[:, 0:1], None, ALU.mult).then_inc(rec_made, 1)
                dve.wait_ge(rec_made, 2 * G + 2)
                dve.wait_ge(y_ready, G + 1)
                dve.scalar_tensor_tensor(xtile(b, t), yb[:, t % 2, 0:D], r, xtile(b, t), ALU.mult, ALU.add).then_inc(x_done, 1)

            dve.memset(masked[:], MASKED).then_inc(consts, 1)
            norm_stats(0)
            for i, n in enumerate("kqv"):
                dve.wait_ge(w_hi_done, i + 1)
                dve.tensor_tensor(w_lo[n][:], w_raw[n][:], w_hi[n][:].bitcast(F32), ALU.subtract).then_inc(w_split, 1)
            norm_apply(0)
            dve.wait_ge(small_in, 48)
            for name in TASKS:
                low_part(name, 0, 0)
            dve.wait_ge(consts, 2)
            b_pair = [0]

            def batch(b, par, last):
                first = isinstance(b, int) and b == 0
                for t in range(TB):
                    G = TB * b + t
                    mask_and_max(G, t, par, b)
                    if t == 0 and not last:
                        norm_stats(b + 1)
                    one, two = SLOTS.get(t, ((), ())) if not last else ((), ())
                    for name in one:
                        low_part(name, b + 1, 1 - par)
                    if not (first and t == 0):
                        pt_low(G - 1, (t - 1) % TB)
                    if t == 0 and not last:
                        norm_apply(b + 1)
                    for name in two:
                        low_part(name, b + 1, 1 - par)
                    if not (first and t < 2):
                        output(G - 2, b - 1 if t < 2 else b, (t - 2) % TB)

            batch(0, 0, False)
            with dve.Fori(0, (NB - 2) // 2) as i:
                b_pair[0] = i
                batch(2 * i + 1, 1, False)
                batch(2 * i + 2, 0, False)
            batch(NB - 1, (NB - 1) % 2, True)
            pt_low(TB * NB - 1, TB - 1)
            output(TB * NB - 2, NB - 1, TB - 2)
            output(TB * NB - 1, NB - 1, TB - 1)

        @block.scalar
        def _(act):
            for i, n in enumerate("kqv"):
                act.wait_ge(w_in, 48)
                act.activation(w_hi[n][:], w_raw[n][:], ACT.Copy).then_inc(w_hi_done, 1)

            def context_high(b):
                act.wait_ge(c_in, 16 * (b + 1))
                ge(act, misc_ready, number(b - 1, "v1"))
                act.activation(c_hi[:], c_raw[:], ACT.Copy).then_inc(c_hi_done, 1)

            def high_part(name, b, par):
                kind, h = name[0], int(name[1])
                bank = TASKS.index(name) % 2
                if kind == "v":
                    act.wait_ge(misc_read, number(b, name))
                    act.activation(v_parts[par][0][:, 2 * h:2 * h + 2, :], v_sum[h][:], ACT.Copy).then_inc(v_hi_done, 1)
                    return
                act.wait_ge(misc_ready, number(b, name))
                if kind == "x":
                    made = act.activation(x_hi[:, h, :], misc[:, bank, :], ACT.Copy)
                else:
                    made = act.activation(parts[kind][par][0][:, h, :], misc[:, bank, :], ACT.Identity, bias=bias[kind][:, h:h + 1])
                made.then_inc(hi_done, 1)

            def exponential(G, t):
                act.wait_ge(bias_ready, G + 1)
                ge(act, pt_ready, G - 1)
                ge(act, rec_made, 2 * (G - 3) - 1)
                act.activation(PM[:, t % 2, :], sc[:, t % 2, :], ACT.Exp, bias=nbias[:, t % 2:t % 2 + 1], scale=SCALE,
                               accum_out=sums[:, t:t + 1]).then_inc(exp_done, 1)

            def pt_high(G, t):
                act.wait_ge(pt_ready, G + 1)
                ge(act, y_ready, G - 1)
                act.activation(pt_hi[t % 2][:], pt[:, t % 2, :], ACT.Copy).then_inc(pt_hi_done, 1)

            context_high(0)
            act.wait_ge(small_in, 48)
            for name in TASKS:
                high_part(name, 0, 0)

            def batch(b, par, last):
                first = isinstance(b, int) and b == 0
                for t in range(TB):
                    G = TB * b + t
                    one, two = SLOTS.get(t, ((), ())) if not last else ((), ())
                    for name in one:
                        high_part(name, b + 1, 1 - par)
                    if not (first and t == 0):
                        pt_high(G - 1, (t - 1) % TB)
                    exponential(G, t)
                    if t == 0 and not last:
                        context_high(b + 1)
                    for name in two:
                        high_part(name, b + 1, 1 - par)
            batches(act, batch)
            pt_high(TB * NB - 1, TB - 1)

        @block.gpsimd
        def _(pool):
            def rstd_of(b):
                pool.wait_ge(stats_ready, b + 1)
                settle(pool, passed)
                pool.tensor_scalar(ve[:], mv[:, :, 1], LN_EPS, None, ALU.add).then_inc(ve_made, 1)
                pool.wait_ge(ve_made, b + 1)
                pool.tensor_tensor(rstd[:], ve[:], mhalf[:], ALU.pow).then_inc(rstd_ready, 1)

            def context_low(b):
                pool.wait_ge(c_hi_done, b + 1)
                pool.tensor_tensor(c_lo[:], c_raw[:], c_hi[:].bitcast(F32), ALU.subtract).then_inc(c_split, 1)

            def v_low(b, par):
                for h in range(2):
                    pool.wait_ge(v_hi_done, 2 * b + h + 1)
                    hi, lo = v_parts[par]
                    pool.tensor_tensor(lo[:, 2 * h:2 * h + 2, :], v_sum[h][:], hi[:, 2 * h:2 * h + 2, :].bitcast(F32), ALU.subtract).then_inc(v_split, 1)

            pool.memset(mhalf[:], -0.5).then_inc(consts, 1)
            pool.wait_ge(consts, 2)
            rstd_of(0)
            context_low(0)
            v_low(0, 0)

            def batch(b, par, last):
                if not last:
                    rstd_of(b + 1)
                    context_low(b + 1)
                    v_low(b + 1, 1 - par)
            batches(pool, batch)


def flamingo_layers(nc, io, out):
    lens = {"A": (14, 16), "B": 46, "D": (11, 18), "E": 28}
    with ExitStack() as stack:
        k = Kit(nc, "all", stack)
        X = k.sb("X", [P, NT, D])
        ident = k.sb("ident", [P, P])
        tg = k.sb("tg", [P, 4])
        x_mid = nc.dram_tensor("x_mid", [NT, P, D], F32).ap()
        x_in, gates_in, zeroed, ident_ready, tanh_done = (k.sem(n) for n in ("x_in", "gates_in", "zeroed", "ident_ready", "tanh_done"))
        with nc.Block() as block:
            @block.sync
            def _(sp):
                sp.dma_start(tg[:, 0:2], io["g_xattn"].partition_broadcast(P)).then_inc(gates_in, 16)
                sp.dma_start(tg[:, 2:4], io["g_ffn"].partition_broadcast(P)).then_inc(gates_in, 16)
                sp.dma_start(X[:, 0:TB, :], io["x"][0].rearrange("(t p) n -> p t n", p=P)).then_inc(x_in, 16)
                sp.wait_ge(x_in, 16)

            @block.scalar
            def _(act):
                act.wait_ge(gates_in, 32)
                act.activation(tg[:], tg[:], ACT.Tanh).then_inc(tanh_done, 1)
                act.wait_ge(tanh_done, 1)

            @block.gpsimd
            def _(pool):
                pool.memset(ident[:], 0.0).then_inc(zeroed, 1)
                pool.wait_ge(zeroed, 1)
                pool.affine_select(out=ident[:], in_=ident[:], compare_op=ALU.not_equal, fill=1.0, base=0,
                                   pattern=[[-1, P]], channel_multiplier=1).then_inc(ident_ready, 1)
                pool.wait_ge(ident_ready, 1)

        def shared(gate):
            return dict(X=X, ident=ident, tg=tg[:, gate:gate + 1], lens=lens)

        def inputs(prefix, **more):
            return dict({n[len(prefix):]: ap for n, ap in io.items() if n.startswith(prefix)}, **more)

        mha_phase(nc, shared(0), "A", inputs("A_", ctxT=io["ctxT"], x=io["x"]), False)
        moe_phase(nc, shared(2), "B", inputs("B_"), 16, 6, True, False)
        xattn_phase(nc, shared(1), "C", inputs("C_", ctxT=io["ctxT"]), x_mid)
        mha_phase(nc, shared(1), "D", inputs("D_"), True)
        moe_phase(nc, shared(3), "E", inputs("E_", x_mid=x_mid), 8, 2, False, True,
                  out.rearrange("b (t p) n -> (b t) p n", p=P))


def kernel(**inputs):
    import numpy as np
    import concourse.bacc as bacc
    from concourse.bass_utils import run_bass_kernel_spmd

    def raw(name):
        return np.asarray(inputs[name])

    def by_partition(a):
        return a.reshape(KC, P).T

    rotated = np.arange(0, 16, 2, dtype=np.float32) / np.float32(16)
    angle = np.arange(S, dtype=np.float32)[:, None] * (np.float32(1) / np.float32(10000) ** rotated)[None, :]
    w_in, b_in = raw("L1_ffn_in_proj_w"), raw("L1_ffn_in_proj_b")
    given = {
        "x": raw("x"), "g_xattn": raw("g_xattn"), "g_ffn": raw("g_ffn"), "ctxT": raw("ctx_1024").transpose(0, 2, 1),
        "A_wq": raw("L0_xattn_Wq").T, "A_wk": raw("L0_xattn_Wk").T, "A_wv": raw("L0_xattn_Wv").T,
        "B_router": raw("L0_ffn_router_w").T, "B_router_b": raw("L0_ffn_router_b"), "B_expert": raw("L0_ffn_expert_w"),
        "C_wq": raw("L1_xattn_q_w").T, "C_wk": raw("L1_xattn_k_w").T, "C_wv": raw("L1_xattn_v_w").T,
        "C_bq": by_partition(raw("L1_xattn_q_b")), "C_bk": by_partition(raw("L1_xattn_k_b")), "C_bv": raw("L1_xattn_v_b"),
        "C_mask": raw("mask_BxSxS2_bk1"),
        "D_wq": w_in[:D].T, "D_wk": w_in[D:2 * D].T, "D_wv": w_in[2 * D:].T, "D_wo": raw("L1_ffn_out_proj_w").T,
        "D_bq": by_partition(b_in[:D]), "D_bk": by_partition(b_in[D:2 * D]), "D_bv": b_in[2 * D:], "D_bo": raw("L1_ffn_out_proj_b"),
        "D_ln_w": raw("L1_ffn_ln1_w"), "D_ln_b": raw("L1_ffn_ln1_b"),
        "D_cos": np.tile(np.cos(angle), (1, 16)), "D_sin": np.tile(np.sin(angle), (1, 16)),
        "E_router": raw("L1_ffn_gate_w").T, "E_router_b": raw("L1_ffn_gate_b"),
        "E_expert": raw("L1_ffn_expert_w").transpose(0, 2, 1), "E_expert_b": raw("L1_ffn_expert_b"),
        "E_ln_w": raw("L1_ffn_ln2_w"), "E_ln_b": raw("L1_ffn_ln2_b"),
    }
    nc = bacc.Bacc("TRN2", target_bir_lowering=False, num_devices=1, dynamic_dma_scratch_size=2048)
    arrays, io = {}, {}
    for name, a in given.items():
        arrays[f"in_{name}_dram"] = np.ascontiguousarray(a)
        io[name] = nc.dram_tensor(f"in_{name}_dram", a.shape, mybir.dt.from_np(a.dtype), kind="ExternalInput").ap()
    out = nc.dram_tensor("out_0_dram", [NB, S, D], F32, kind="ExternalOutput").ap()
    flamingo_layers(nc, io, out)
    r = run_bass_kernel_spmd(nc, [arrays], core_ids=[0])
    return r.results[0]["out_0_dram"]
```
